# Optimizing a Trainium2 kernel written in Bass

```python
import numpy as np
import jax
import jax.numpy as jnp

def _softmax(x, axis=-1):
    return jax.nn.softmax(x, axis=axis)

def _gelu(x):
    return jax.nn.gelu(x, approximate=True)

def _silu(x):
    return jax.nn.silu(x)

def _sigmoid(x):
    return jax.nn.sigmoid(x)

def _layernorm(x, axis=-1, eps=1e-05):
    m = jnp.mean(x, axis=axis, keepdims=True)
    v = jnp.var(x, axis=axis, keepdims=True)
    return (x - m) / jnp.sqrt(v + eps)

def _scatter_add(tgt, idx, src, axis=0):
    return tgt.at[idx].add(src)

def _segment_sum(src, seg, n):
    return jax.ops.segment_sum(src, seg, n)
kernel_name = 'mk_early_fusion_embed_d2_tok_img1024_r4_9e9d65'

def setup_inputs(seed: int=0):
    np.random.seed(seed)
    _w = jnp.asarray

    def _rec_inputs():
        import jax
        import jax.numpy as jnp
        _rk = jax.random.key(seed)
        x = -4.65018e-05 + 0.999886 * jax.random.normal(jax.random.fold_in(_rk, 1), (32, 3, 128, 128), jnp.float32)
        x_txt = jax.random.randint(jax.random.fold_in(_rk, 51), (32, 128), 0, 12564, jnp.int32)
        return (x, x_txt)
    x, x_txt = _rec_inputs()

    def _L0_tok_setup():
        import jax, jax.numpy as jnp
        import numpy as np
        P = 16
        key = jax.random.key(seed)
        k1, k2, k3 = jax.random.split(key, 3)
        B, C, H, W_ = (64, 3, 128, 128)
        D = 256
        x = jax.random.normal(k1, (B, C, H, W_), dtype=jnp.float32)
        W = jax.random.normal(k2, (C * P * P, D), dtype=jnp.float32) * (1.0 / np.sqrt(C * P * P))
        b = jax.random.normal(k3, (D,), dtype=jnp.float32) * 0.01
        return {'x': x, 'W': W, 'b': b}
    _L0_tok_all = _L0_tok_setup()
    _L0_tok_in = {k: v for k, v in _L0_tok_all.items() if k in ('W', 'b')}
    del _L0_tok_all

    def _L0_txt_setup():
        import jax, jax.numpy as jnp
        import numpy as np
        VOCAB = 50257
        DIM = 256
        PADDING_IDX = 0
        key = jax.random.key(seed)
        k_w, k_ids = jax.random.split(key)
        weight = jax.random.normal(k_w, (VOCAB, DIM), dtype=jnp.float32)
        weight = weight.at[PADDING_IDX].set(0.0)
        input_ids = jax.random.randint(k_ids, (16, 512), 0, VOCAB, dtype=jnp.int64)
        return {'weight': weight, 'input_ids': input_ids}
    _L0_txt_all = _L0_txt_setup()
    _L0_txt_in = {k: v for k, v in _L0_txt_all.items() if k in ('weight',)}
    del _L0_txt_all

    def _L0_attn_setup():
        import jax, jax.numpy as jnp
        import numpy as np
        import math
        D_MODEL = 256
        MAX_SEQ_LEN = 512
        BATCH = 4
        SEQ_LEN = 512
        key = jax.random.key(seed)
        kx, kq, kk, kv = jax.random.split(key, 4)
        x = jax.random.normal(kx, (BATCH, SEQ_LEN, D_MODEL), dtype=jnp.float32)
        s = 1.0 / math.sqrt(D_MODEL)
        wq = jax.random.uniform(kq, (D_MODEL, D_MODEL), dtype=jnp.float32, minval=-s, maxval=s)
        wk = jax.random.uniform(kk, (D_MODEL, D_MODEL), dtype=jnp.float32, minval=-s, maxval=s)
        wv = jax.random.uniform(kv, (D_MODEL, D_MODEL), dtype=jnp.float32, minval=-s, maxval=s)
        return {'x': x, 'wq': wq, 'wk': wk, 'wv': wv}
    _L0_attn_all = _L0_attn_setup()
    _L0_attn_in = {k: v for k, v in _L0_attn_all.items() if k in ('wq', 'wk', 'wv')}
    del _L0_attn_all

    def _L0_ffn_setup():
        import jax, jax.numpy as jnp
        import numpy as np
        EPS = 1e-08

        def _ternary_linear(x, w):
            alpha = jnp.mean(jnp.abs(w))
            w_t = jnp.sign(w) * (jnp.abs(w) > 0.5 * alpha).astype(w.dtype)
            w_q = w + jax.lax.stop_gradient(w_t - w)
            d = x.shape[-1]
            rms = jnp.sqrt(jnp.sum(x * x, axis=-1, keepdims=True)) / jnp.sqrt(jnp.asarray(d, x.dtype))
            x_norm = x / (rms + EPS)
            return jnp.einsum('bsd,fd->bsf', x_norm, w_q)
        key = jax.random.key(seed)
        k1, k2, k3 = jax.random.split(key, 3)
        d_model, d_ff = (256, 1024)
        B, S = (4, 1024)
        x = jax.random.normal(k1, (B, S, d_model), dtype=jnp.float32)
        w_up = jax.random.normal(k2, (d_ff, d_model), dtype=jnp.float32) * 0.02
        w_down = jax.random.normal(k3, (d_model, d_ff), dtype=jnp.float32) * 0.02
        return {'x': x, 'w_up': w_up, 'w_down': w_down}
    _L0_ffn_all = _L0_ffn_setup()
    _L0_ffn_in = {k: v for k, v in _L0_ffn_all.items() if k in ('w_up', 'w_down')}
    del _L0_ffn_all

    def _L1_attn_setup():
        import jax, jax.numpy as jnp
        import numpy as np
        D_MODEL = 256
        EXPAND = 2
        D_INNER = D_MODEL * EXPAND
        C = 8
        B, T = (4, 512)
        key = jax.random.key(seed)
        ks = jax.random.split(key, 8)
        x = jax.random.normal(ks[0], (B, T, D_MODEL), jnp.float32)
        a = np.log(1.0 / np.exp(np.log(0.999) / C) - 1.0)
        b = np.log(1.0 / np.exp(np.log(0.9) / C) - 1.0)
        omega = (a + (b - a) * jax.random.uniform(ks[1], (1, 1, D_INNER))).astype(jnp.float32)
        s = 0.02
        Win = (jax.random.normal(ks[2], (2 * D_INNER, D_MODEL)) * s).astype(jnp.float32)
        Wl = (jax.random.normal(ks[3], (D_INNER, D_INNER)) * s).astype(jnp.float32)
        bl = jnp.zeros((D_INNER,), jnp.float32)
        Wv = (jax.random.normal(ks[4], (D_INNER, D_INNER)) * s).astype(jnp.float32)
        bv = jnp.zeros((D_INNER,), jnp.float32)
        Wout = (jax.random.normal(ks[5], (D_MODEL, D_INNER)) * s).astype(jnp.float32)
        return dict(x=x, omega=omega, Win=Win, Wl=Wl, bl=bl, Wv=Wv, bv=bv, Wout=Wout)
    _L1_attn_all = _L1_attn_setup()
    _L1_attn_in = {k: v for k, v in _L1_attn_all.items() if k in ('omega', 'Win', 'Wl', 'bl', 'Wv', 'bv', 'Wout')}
    del _L1_attn_all

    def _L1_ffn_setup():
        import jax, jax.numpy as jnp
        import numpy as np
        NUM_EXPERTS = 8
        HIDDEN = 256
        INTER = 256
        BATCH = 2
        SEQ = 256
        TOP_K = 2
        SWIGLU_ALPHA = 1.702
        LIMIT = 7.0

        def _grouped_mm(x, w, expert_ids):
            onehot = jax.nn.one_hot(expert_ids, w.shape[0], dtype=x.dtype)
            y_all = jnp.einsum('tk,ekn->etn', x, w)
            return jnp.einsum('te,etn->tn', onehot, y_all)

        def _gpt_oss_swiglu(x):
            gate = jnp.minimum(x[..., ::2], LIMIT)
            up = jnp.clip(x[..., 1::2], -LIMIT, LIMIT)
            glu = gate * jax.nn.sigmoid(gate * SWIGLU_ALPHA)
            return (up + 1.0) * glu
        key = jax.random.key(seed)
        ks = jax.random.split(key, 7)
        hidden_states = jax.random.normal(ks[0], (BATCH, SEQ, HIDDEN), jnp.float32)
        router_indices = jax.random.randint(ks[1], (BATCH * SEQ, TOP_K), 0, NUM_EXPERTS)
        routing_weights = jax.nn.softmax(jax.random.normal(ks[2], (BATCH * SEQ, NUM_EXPERTS), jnp.float32), axis=-1)
        scale = 0.02
        gate_up_proj = jax.random.normal(ks[3], (NUM_EXPERTS, HIDDEN, 2 * INTER), jnp.float32) * scale
        gate_up_proj_bias = jax.random.normal(ks[4], (NUM_EXPERTS, 2 * INTER), jnp.float32) * scale
        down_proj = jax.random.normal(ks[5], (NUM_EXPERTS, INTER, HIDDEN), jnp.float32) * scale
        down_proj_bias = jax.random.normal(ks[6], (NUM_EXPERTS, HIDDEN), jnp.float32) * scale
        return {'hidden_states': hidden_states, 'router_indices': router_indices, 'routing_weights': routing_weights, 'gate_up_proj': gate_up_proj, 'gate_up_proj_bias': gate_up_proj_bias, 'down_proj': down_proj, 'down_proj_bias': down_proj_bias}
    _L1_ffn_all = _L1_ffn_setup()
    _L1_ffn_in = {k: v for k, v in _L1_ffn_all.items() if k in ('router_indices', 'routing_weights', 'gate_up_proj', 'gate_up_proj_bias', 'down_proj', 'down_proj_bias')}
    del _L1_ffn_all
    return {'x': x, 'x_txt': x_txt, 'L0_tok_W': _L0_tok_in['W'], 'L0_tok_b': _L0_tok_in['b'], 'L0_txt_weight': _L0_txt_in['weight'], 'L0_attn_wq': _L0_attn_in['wq'], 'L0_attn_wk': _L0_attn_in['wk'], 'L0_attn_wv': _L0_attn_in['wv'], 'L0_ffn_w_up': _L0_ffn_in['w_up'], 'L0_ffn_w_down': _L0_ffn_in['w_down'], 'L1_attn_omega': _L1_attn_in['omega'], 'L1_attn_Win': _L1_attn_in['Win'], 'L1_attn_Wl': _L1_attn_in['Wl'], 'L1_attn_bl': _L1_attn_in['bl'], 'L1_attn_Wv': _L1_attn_in['Wv'], 'L1_attn_bv': _L1_attn_in['bv'], 'L1_attn_Wout': _L1_attn_in['Wout'], 'L1_ffn_router_indices': _L1_ffn_in['router_indices'], 'L1_ffn_routing_weights': _L1_ffn_in['routing_weights'], 'L1_ffn_gate_up_proj': _L1_ffn_in['gate_up_proj'], 'L1_ffn_gate_up_proj_bias': _L1_ffn_in['gate_up_proj_bias'], 'L1_ffn_down_proj': _L1_ffn_in['down_proj'], 'L1_ffn_down_proj_bias': _L1_ffn_in['down_proj_bias']}

def reference(x, x_txt, L0_tok_W, L0_tok_b, L0_txt_weight, L0_attn_wq, L0_attn_wk, L0_attn_wv, L0_ffn_w_up, L0_ffn_w_down, L1_attn_omega, L1_attn_Win, L1_attn_Wl, L1_attn_bl, L1_attn_Wv, L1_attn_bv, L1_attn_Wout, L1_ffn_router_indices, L1_ffn_routing_weights, L1_ffn_gate_up_proj, L1_ffn_gate_up_proj_bias, L1_ffn_down_proj, L1_ffn_down_proj_bias):
    import jax
    import jax.numpy as jnp

    def _L0_tok_ref(x, W, b):
        import jax, jax.numpy as jnp
        import numpy as np
        P = 16
        B, C, H, W_ = x.shape
        nh, nw = (H // P, W_ // P)
        patches = x.reshape(B, C, nh, P, nw, P)
        patches = patches.transpose(0, 2, 4, 1, 3, 5)
        patches = patches.reshape(B, nh * nw, C * P * P)
        return jnp.einsum('bnk,kd->bnd', patches, W) + b

    def _L0_txt_ref(weight, input_ids):
        import jax, jax.numpy as jnp
        import numpy as np
        VOCAB = 50257
        DIM = 256
        PADDING_IDX = 0
        return jnp.take(weight, input_ids, axis=0)

    def _L0_attn_ref(x, wq, wk, wv):
        import jax, jax.numpy as jnp
        import numpy as np
        import math
        D_MODEL = 256
        MAX_SEQ_LEN = 512
        BATCH = 4
        SEQ_LEN = 512
        q = jnp.einsum('bsd,ed->bse', x, wq)
        k = jnp.einsum('bsd,ed->bse', x, wk)
        v = jnp.einsum('bsd,ed->bse', x, wv)
        scale = 1.0 / math.sqrt(q.shape[-1])
        scores = jnp.einsum('bqd,bkd->bqk', q, k) * scale
        seq_len = x.shape[1]
        causal = jnp.tril(jnp.ones((seq_len, seq_len), dtype=bool))
        scores = jnp.where(causal[None, :, :], scores, -jnp.inf)
        attn = jax.nn.softmax(scores, axis=-1)
        return jnp.einsum('bqk,bkd->bqd', attn, v)

    def _L0_ffn_ref(x, w_up, w_down):
        import jax, jax.numpy as jnp
        import numpy as np
        EPS = 1e-08

        def _ternary_linear(x, w):
            alpha = jnp.mean(jnp.abs(w))
            w_t = jnp.sign(w) * (jnp.abs(w) > 0.5 * alpha).astype(w.dtype)
            w_q = w + jax.lax.stop_gradient(w_t - w)
            d = x.shape[-1]
            rms = jnp.sqrt(jnp.sum(x * x, axis=-1, keepdims=True)) / jnp.sqrt(jnp.asarray(d, x.dtype))
            x_norm = x / (rms + EPS)
            return jnp.einsum('bsd,fd->bsf', x_norm, w_q)
        h = jax.nn.gelu(_ternary_linear(x, w_up), approximate=False)
        return _ternary_linear(h, w_down)

    def _L1_attn_ref(x, omega, Win, Wl, bl, Wv, bv, Wout):
        import jax, jax.numpy as jnp
        import numpy as np
        D_MODEL = 256
        EXPAND = 2
        D_INNER = D_MODEL * EXPAND
        C = 8
        B, T = (4, 512)
        xz = jnp.einsum('btd,ed->bte', x, Win)
        xi, z = jnp.split(xz, 2, axis=-1)
        log_lam = -C * jax.nn.softplus(omega) * jax.nn.sigmoid(jnp.einsum('bti,ji->btj', xi, Wl) + bl)
        lam = jnp.exp(log_lam)
        v = jnp.einsum('bti,ji->btj', xi, Wv) + bv
        h0 = xi[:, 0]

        def step(h_prev, inp):
            x_t, v_t, lam_t = inp
            vh = jnp.sum(v_t * h_prev, axis=-1, keepdims=True)
            vv = jnp.sum(v_t * v_t, axis=-1, keepdims=True)
            Qh = h_prev - 2.0 * v_t * (vh / vv)
            h = lam_t * Qh + (1.0 - lam_t) * x_t
            return (h, h)
        xs = (jnp.swapaxes(xi[:, 1:], 0, 1), jnp.swapaxes(v[:, 1:], 0, 1), jnp.swapaxes(lam[:, 1:], 0, 1))
        _, hs = jax.lax.scan(step, h0, xs)
        h = jnp.concatenate([h0[:, None], jnp.swapaxes(hs, 0, 1)], axis=1)
        return jnp.einsum('bti,di->btd', jax.nn.silu(z) * h, Wout)

    def _L1_ffn_ref(hidden_states, router_indices, routing_weights, gate_up_proj, gate_up_proj_bias, down_proj, down_proj_bias):
        import jax, jax.numpy as jnp
        import numpy as np
        NUM_EXPERTS = 8
        HIDDEN = 256
        INTER = 256
        BATCH = 2
        SEQ = 256
        TOP_K = 2
        SWIGLU_ALPHA = 1.702
        LIMIT = 7.0

        def _grouped_mm(x, w, expert_ids):
            onehot = jax.nn.one_hot(expert_ids, w.shape[0], dtype=x.dtype)
            y_all = jnp.einsum('tk,ekn->etn', x, w)
            return jnp.einsum('te,etn->tn', onehot, y_all)

        def _gpt_oss_swiglu(x):
            gate = jnp.minimum(x[..., ::2], LIMIT)
            up = jnp.clip(x[..., 1::2], -LIMIT, LIMIT)
            glu = gate * jax.nn.sigmoid(gate * SWIGLU_ALPHA)
            return (up + 1.0) * glu
        B = hidden_states.shape[0]
        H = hidden_states.shape[-1]
        x = hidden_states.reshape(-1, H)
        M = x.shape[0]
        top_k = router_indices.shape[1]
        num_experts = gate_up_proj.shape[0]
        topk_weights = jnp.take_along_axis(routing_weights, router_indices, axis=1)
        flat_experts = router_indices.reshape(-1)
        sort_idx = jnp.argsort(flat_experts)
        sorted_pos = sort_idx // top_k
        expert_sorted = flat_experts[sort_idx]
        grouped = x[sorted_pos]
        gate_up = _grouped_mm(grouped, gate_up_proj, expert_sorted)
        gate_up = gate_up + gate_up_proj_bias[expert_sorted]
        inter = _gpt_oss_swiglu(gate_up)
        down = _grouped_mm(inter, down_proj, expert_sorted)
        down = down + down_proj_bias[expert_sorted]
        down = down * topk_weights.reshape(-1)[sort_idx][:, None]
        out = jnp.zeros((M, H), x.dtype).at[sorted_pos].add(down)
        return out.reshape(B, -1, H)
    h = _L0_tok_ref(x, L0_tok_W, L0_tok_b)
    h = jnp.concatenate([h, _L0_txt_ref(L0_txt_weight, x_txt)], axis=1)
    h = h + _L0_attn_ref(_layernorm(h, axis=-1), L0_attn_wq, L0_attn_wk, L0_attn_wv)
    h = h + _L0_ffn_ref(_layernorm(h, axis=-1), L0_ffn_w_up, L0_ffn_w_down)
    h = h + _L1_attn_ref(_layernorm(h, axis=-1), L1_attn_omega, L1_attn_Win, L1_attn_Wl, L1_attn_bl, L1_attn_Wv, L1_attn_bv, L1_attn_Wout)
    h = h + _L1_ffn_ref(_layernorm(h, axis=-1), L1_ffn_router_indices, L1_ffn_routing_weights, L1_ffn_gate_up_proj, L1_ffn_gate_up_proj_bias, L1_ffn_down_proj, L1_ffn_down_proj_bias)
    return h

_drawn_inputs = setup_inputs


def setup_inputs(seed=0):
    import zlib

    import numpy as np

    out = dict(_drawn_inputs(seed))
    spreads = {'L1_attn_bl': (0.0, 0.8), 'L1_attn_bv': (0.0, 2.0)}
    factors = {'L0_tok_b': 7.635,
     'L1_attn_omega': 8.0,
     'L1_attn_Win': 8.0,
     'L1_attn_Wl': 8.0,
     'L1_attn_Wv': 8.0,
     'L1_attn_Wout': 8.0,
     'L1_ffn_routing_weights': 8.0,
     'L1_ffn_gate_up_proj': 8.0,
     'L1_ffn_gate_up_proj_bias': 22.311,
     'L1_ffn_down_proj': 8.0,
     'L1_ffn_down_proj_bias': 64.0}
    for name, (base, spread) in spreads.items():
        noise = np.random.default_rng([zlib.crc32(name.encode()), seed]).standard_normal(out[name].shape)
        drawn = base * np.exp(spread * noise) if base else spread * noise
        out[name] = jnp.asarray(drawn.astype(out[name].dtype))
    for name, factor in factors.items():
        out[name] = (out[name] * factor).astype(out[name].dtype)
    return out
```

```python
from contextlib import ExitStack

import concourse.bass as bass
from concourse import mybir

ALU = mybir.AluOpType
ACT = mybir.ActivationFunctionType
F32 = mybir.dt.float32
F32R = mybir.dt.float32r
I32 = mybir.dt.int32
U32 = mybir.dt.uint32
AX_X = mybir.AxisListType.X

P = 128
NB = 32
D = 256
DC = D // P
N_IMG = 64
N_TXT = 128
T = N_IMG + N_TXT
KP = 3 * 16 * 16
KPC = KP // P
FF = 1024
FC = FF // P
G = NB // 2
TILES = 3
GT = TILES * P
DI = 512
IC = DI // P
STEPS = 16
BLOCKS = T // STEPS
BT = STEPS * NB
BTILES = BT // P
C_DECAY = 8.0
LN_EPS = 1e-5
RMS_EPS = 1e-8
MASKED = -3.0e38
E_N = 8
MT = 512
LIMIT = 7.0
ALPHA = 1.702


def wait(eng, sem, count):
    if isinstance(count, int) and count <= 0:
        return
    eng.wait_ge(sem, count)


def settle(eng):
    eng.nop(nofuse=True)


class Names:
    pass


def part_a(nc, W, io, consts):
    with ExitStack() as ctx:
        def sb(name, shape, dt=F32):
            return ctx.enter_context(nc.sbuf_tensor(name, shape, dt))

        def sem(name):
            return ctx.enter_context(nc.semaphore(name))

        stage = sb("weight_stage", [P, 4 * DI])
        absum, abparts = sb("abs_sum", [P, 4]), sb("abs_sum_parts", [P, 32])
        half_alpha = sb("half_alpha", [P, 2])
        tern_tmp = sb("ternary_tmp", [P, 1024])
        bias_tok = sb("patch_bias", [P, D])
        ids = sb("text_ids", [P, 2, 2], I32)
        tok_h, tok_l = sb("tokW_hi", [P, KPC, D], F32R), sb("tokW_lo", [P, KPC, D], F32R)
        wq, wk = sb("wq", [P, DC, D]), sb("wk", [P, DC, D])
        qk_h, qk_l = sb("qk_hi", [P, DC, D], F32R), sb("qk_lo", [P, DC, D], F32R)
        wv_h, wv_l = sb("wv_hi", [P, DC, D], F32R), sb("wv_lo", [P, DC, D], F32R)
        up_w = sb("ternary_up", [P, DC, FF], F32R)
        dn_w = sb("ternary_down", [P, FC, D], F32R)
        mask = sb("causal_mask", [P, TILES, D])
        patches = sb("patches", [P, KPC, P])
        pat_h, pat_l = sb("patches_hi", [P, KPC, P], F32R), sb("patches_lo", [P, KPC, P], F32R)
        emb = sb("embedded", [P, 2, TILES, D])
        stats, moments = sb("ln_stats", [P, TILES, 6]), sb("ln_moments", [P, TILES, 2])
        ve, rstd = sb("ln_var_eps", [P, TILES]), sb("ln_rstd", [P, TILES])
        xn = sb("x_normed", [P, TILES, D])
        xT_h, xT_l = sb("xT_hi", [P, DC, GT], F32R), sb("xT_lo", [P, DC, GT], F32R)
        tT_h, tT_l = sb("tT_hi", [P, DC, GT], F32R), sb("tT_lo", [P, DC, GT], F32R)
        v_h, v_l = sb("v_hi", [P, TILES, D], F32R), sb("v_lo", [P, TILES, D], F32R)
        prob = sb("probs", [P, TILES, D])
        rowmax, negmax = sb("row_max", [P, TILES]), sb("neg_max", [P, TILES])
        rowsum, rinv = sb("row_sum", [P, TILES]), sb("row_inv", [P, TILES])
        pT_h, pT_l = sb("probT_hi", [P, 5, P], F32R), sb("probT_lo", [P, 5, P], F32R)
        h = sb("residual", [P, 2, TILES, D])
        stats2, moments2 = sb("ln2_stats", [P, TILES, 6]), sb("ln2_moments", [P, TILES, 2])
        pair, roots = sb("ln2_pair", [P, 2, TILES]), sb("ln2_roots", [P, 2, TILES])
        den2, scale2 = sb("ln2_den", [P, TILES]), sb("ln2_scale", [P, TILES])
        xn2 = sb("x2_normed", [P, TILES, D])
        x2_h, x2_l = sb("x2T_hi", [P, DC, GT], F32R), sb("x2T_lo", [P, DC, GT], F32R)
        act = sb("gelu_out", [P, 2, GT])
        sq = sb("gelu_sq", [P, 2, GT])
        sqsum = sb("gelu_sq_sum", [P, GT])
        act_h, act_l = sb("gelu_hi", [P, FC, GT], F32R), sb("gelu_lo", [P, FC, GT], F32R)
        ms, rms = sb("rms_mean", [P, TILES]), sb("rms_root", [P, TILES])
        rden, rscale = sb("rms_den", [P, TILES]), sb("rms_scale", [P, TILES])
        ps = ctx.enter_context(nc.psum_tensor("psA", [P, 8, 512], F32))
        XT = ps[:, 0:2, :]
        SC = ps[:, 2:4, :].rearrange("p a b -> p (a b)")
        VO = ps[:, 4:6, :].rearrange("p a b -> p (a b)")
        ident, ones, halfpow = consts.ident, consts.ones, consts.halfpow

        s = {}
        for name in """tern_in stage_in0 stage_in1 ids_in0 ids_in1 w_hi w_lo w_abs_parts w_abs w_alpha w_alpha_ps w_sum w_sign const_in mask_zero mask_ready
                merge_ps qk_in qk_ready
                patch_in patch_hi patch_lo tok_done emb_img text_in0 text_in1 ln_stats ln_aggr ln_ve ln_rstd ln_out xT_done
                x_hi x_lo t_done t_hi t_lo v_done v_hi v_lo score_done max_done negmax_done exp_done pT_done pT_hi
                pT_lo pv_done rinv_done h1_done ln2_stats ln2_aggr ln2_pair ln2_roots ln2_den ln2_scale ln2_out
                x2T_done x2_hi x2_lo up_done gelu_done sq_done ffn_hi ffn_lo sqsum_done ss_done ms_done rms_done
                rden_done rscale_done down_done h2_done stored""".split():
            s[name] = sem("A_" + name)

        def flat(t):
            return t[:].rearrange("p a b -> p (a b)")

        chunks = []
        for src, hi, lo in ((io["tokW"], tok_h, tok_l), (io["wvT"], wv_h, wv_l), (io["WinT"], W.in_h, W.in_l),
                            (io["WlT"], W.l_h, W.l_l), (io["WvT"], W.v_h, W.v_l), (io["WoutT"], W.out_h, W.out_l)):
            cols = flat(hi).shape[1]
            for a in range(0, cols, 1024):
                b = min(cols, a + 1024)
                chunks.append((src[:, a:b], flat(hi)[:, a:b], flat(lo)[:, a:b], b - a))
        n_split = len(chunks)
        tern = [(io["upT"], 0, flat(up_w)), (io["downT"], 1, flat(dn_w))]

        block = ctx.enter_context(nc.Block())

        def run(eng, step):
            for g in (-2, -1, 0, 1):
                step(g, g % 2, g // 2)
            with eng.Fori(1, G // 2 - 2) as pair_:
                step(2 * pair_, 0, pair_)
                step(2 * pair_ + 1, 1, pair_)
            for g in range(G - 4, G):
                step(g, g % 2, g // 2)

        def has(g, k):
            return not isinstance(g, int) or 0 <= g + k < G

        stage_in = [s["stage_in0"], s["stage_in1"]]
        text_in = [s["text_in0"], s["text_in1"]]
        ids_in = [s["ids_in0"], s["ids_in1"]]
        stage_half = [stage[:, 0:1024], stage[:, 1024:2048]]

        @block.sync
        def _(sp):
            sp.dma_start(bias_tok[:], io["tokb"]).then_inc(s["const_in"], 16)
            sp.dma_start(wq[:], io["wq"]).then_inc(s["qk_in"], 16)
            sp.dma_start(wk[:], io["wk"]).then_inc(s["qk_in"], 16)
            for n, (src, _, _) in enumerate(tern):
                if n:
                    sp.wait_ge(s["w_sum"], 2 * n)
                sp.dma_start(stage[:], src).then_inc(s["tern_in"], 16)
            sp.wait_ge(s["w_sum"], 4)
            for n, (src, _, _, cols) in enumerate(chunks):
                if n >= 2:
                    sp.wait_ge(s["w_lo"], n - 1)
                sp.dma_start(stage_half[n % 2][:, 0:cols], src).then_inc(stage_in[n % 2], 16)
            for k in range(2):
                sp.dma_start(ids[:, k, :], io["ids"][k]).then_inc(ids_in[k], 16)

            def step(g, sl, pr):
                if has(g, 2):
                    wait(sp, s["patch_lo"], g + 2)
                    wait(sp, s["patch_hi"], g + 2)
                    sp.dma_start(patches[:], io["patches"][g + 2]).then_inc(s["patch_in"], 16)
                if has(g, 3) and has(g, 1):
                    sp.wait_ge(text_in[1 - sl], 32 * (pr + 1 + sl))
                    sp.dma_start(ids[:, 1 - sl, :], io["ids"][g + 3]).then_inc(ids_in[1 - sl], 16)
                if has(g, 0):
                    sp.wait_ge(s["h2_done"], g + 1)
                    for j in range(2):
                        sp.dma_start(io["h2"][2 * g + j, 0:N_IMG, :],
                                     h[j * N_IMG:(j + 1) * N_IMG, sl, 0, :]).then_inc(s["stored"], 16)
                        sp.dma_start(io["h2"][2 * g + j, N_IMG:T, :], h[:, sl, 1 + j, :]).then_inc(s["stored"], 16)

            run(sp, step)
            sp.wait_ge(s["stored"], 64 * G)

        @block.gpsimd
        def _(pool):
            nc.gpsimd.memset(mask[:], 0.0).then_inc(s["mask_zero"], 1)
            pool.wait_ge(s["mask_zero"], 1)
            nc.gpsimd.affine_select(out=mask[:, 0, :], in_=mask[:, 0, :], compare_op=ALU.is_ge, fill=MASKED,
                                    base=0, pattern=[[-1, D]], channel_multiplier=1).then_inc(s["mask_zero"], 1)
            pool.wait_ge(s["mask_zero"], 2)
            nc.gpsimd.affine_select(out=mask[:, 0, 0:N_IMG], in_=mask[:, 0, 0:N_IMG], compare_op=ALU.is_ge,
                                    fill=MASKED, base=N_IMG - 1, pattern=[[0, N_IMG]],
                                    channel_multiplier=-1).then_inc(s["mask_zero"], 1)
            nc.gpsimd.memset(mask[:, 1, N_IMG:2 * N_IMG], MASKED)
            nc.gpsimd.memset(mask[:, 2, 0:N_IMG], MASKED)
            nc.gpsimd.affine_select(out=mask[:, 1:3, P:2 * P], in_=mask[:, 1:3, P:2 * P], compare_op=ALU.is_ge,
                                    fill=MASKED, base=0, pattern=[[0, 2], [-1, P]],
                                    channel_multiplier=1).then_inc(s["mask_ready"], 1)

            def gathers(g, sl, half):
                pool.wait_ge(ids_in[sl], 16 * (half + 1))
                wait(pool, s["h1_done"], g - 1)
                settle(pool)
                for j in range(2):
                    pool.indirect_dma_start(
                        emb[:, sl, 1 + j, :], None, io["table"],
                        bass.IndirectOffsetOnAxis(ap=ids[:, sl, j:j + 1], axis=0),
                    ).then_inc(text_in[sl], 16)

            def root_ln(g):
                pool.wait_ge(s["ln_aggr"], g + 1)
                settle(pool)
                nc.gpsimd.tensor_scalar(ve[:], moments[:, :, 1], LN_EPS, None, ALU.add).then_inc(s["ln_ve"], 1)
                pool.wait_ge(s["ln_ve"], g + 1)
                wait(pool, s["ln_out"], g)
                nc.gpsimd.tensor_tensor(rstd[:], ve[:], halfpow[:, 1, 0:TILES], ALU.pow).then_inc(s["ln_rstd"], 1)

            def step(g, sl, pr):
                def chunk_lo(c):
                    k = FC * g + c
                    pool.wait_ge(s["ffn_hi"], k + 1)
                    nc.gpsimd.tensor_tensor(act_l[:, c, :], act[:, c % 2, :], act_h[:, c, :].bitcast(F32),
                                            ALU.subtract).then_inc(s["ffn_lo"], 1)

                if has(g, 0):
                    for c in range(4):
                        chunk_lo(c)
                if has(g, 2):
                    pool.wait_ge(s["patch_hi"], g + 3)
                    nc.gpsimd.tensor_tensor(pat_l[:], patches[:], pat_h[:].bitcast(F32),
                                            ALU.subtract).then_inc(s["patch_lo"], 1)
                if has(g, 0):
                    for c in range(4, FC):
                        chunk_lo(c)
                if has(g, 2):
                    root_ln(g + 2)
                if has(g, 0):
                    pool.wait_ge(s["ms_done"], g + 1)
                    wait(pool, s["rden_done"], g)
                    nc.gpsimd.tensor_tensor(rms[:], ms[:], halfpow[:, 0, 0:TILES], ALU.pow).then_inc(s["rms_done"], 1)
                if has(g, 1):
                    pool.wait_ge(s["ln2_aggr"], g + 2)
                    settle(pool)
                    nc.gpsimd.tensor_scalar(pair[:, 0, :], moments2[:, :, 1], 0.0, None, ALU.add)
                    nc.gpsimd.tensor_scalar(pair[:, 1, :], moments2[:, :, 1], LN_EPS, None,
                                            ALU.add).then_inc(s["ln2_pair"], 1)
                    pool.wait_ge(s["ln2_pair"], g + 2)
                    nc.gpsimd.tensor_tensor(roots[:], pair[:], halfpow[:, 0:1, 0:TILES].to_broadcast([P, 2, TILES]),
                                            ALU.pow).then_inc(s["ln2_roots"], 1)
                if has(g, 3):
                    gathers(g + 3, 1 - sl, pr + sl + 1)

            gathers(0, 0, 0)
            run(pool, step)

        @block.scalar
        def _(sc):
            for n, (_, hi, _, cols) in enumerate(chunks):
                sc.wait_ge(stage_in[n % 2], 16 * (n // 2 + 1))
                nc.scalar.activation(hi, stage_half[n % 2][:, 0:cols], ACT.Copy).then_inc(s["w_hi"], 1)
            sc.wait_ge(s["merge_ps"], 1)
            nc.scalar.activation(qk_h[:], SC[:, 0:DC * D].rearrange("p (a b) -> p a b", a=DC), ACT.Copy,
                                 scale=float(D) ** -0.5).then_inc(s["qk_ready"], 1)

            def gelu(g, c):
                k = FC * g + c
                sc.wait_ge(s["up_done"], k + 1)
                wait(sc, s["ffn_lo"], k - 1)
                wait(sc, s["sq_done"], k - 1)
                nc.scalar.activation(act[:, c % 2, :], ps[:, 6 + c % 2, 0:GT], ACT.Gelu).then_inc(s["gelu_done"], 1)
                sc.wait_ge(s["gelu_done"], k + 1)
                if c == 0:
                    wait(sc, s["ss_done"], g)
                    out = sqsum[:]
                else:
                    wait(sc, s["sqsum_done"], (FC - 1) * g + c - 2)
                    out = sq[:, c % 2, :]
                nc.scalar.activation(out, act[:, c % 2, :], ACT.Square).then_inc(s["sq_done"], 1)

            def hi(out, in_, done, got, freed, g):
                sc.wait_ge(got, g + 1)
                wait(sc, freed, g)
                nc.scalar.activation(out, in_, ACT.Copy).then_inc(done, 1)

            def step(g, sl, pr):
                n = g + 1
                if has(g, 1):
                    hi(xT_h[:], XT[:, :, 0:GT], s["x_hi"], s["xT_done"], s["score_done"], n)
                if has(g, 0):
                    for c in range(4):
                        gelu(g, c)
                if has(g, 1):
                    hi(tT_h[:], ps[:, 2:4, 0:GT], s["t_hi"], s["t_done"], s["score_done"], n)
                    hi(v_h[:], VO[:, 0:TILES * D].rearrange("p (a b) -> p a b", a=TILES), s["v_hi"], s["v_done"], s["pv_done"], n)
                if has(g, 0):
                    for c in range(4, FC):
                        gelu(g, c)
                if has(g, 1):
                    sc.wait_ge(s["negmax_done"], n + 1)
                    wait(sc, s["rinv_done"], n)
                    for i in range(TILES):
                        last = nc.scalar.activation(prob[:, i, :], prob[:, i, :], ACT.Exp, bias=negmax[:, i:i + 1],
                                                    accum_out=rowsum[:, i:i + 1])
                    last.then_inc(s["exp_done"], 1)
                    hi(pT_h[:], ps[:, 0:2, :].rearrange("p a b -> p (a b)")[:, 0:5 * P]
                       .rearrange("p (a b) -> p a b", a=5), s["pT_hi"], s["pT_done"], s["pv_done"], n)
                    sc.wait_ge(s["x2T_done"], n + 1)
                    wait(sc, s["up_done"], FC * n)
                    nc.scalar.activation(x2_h[:], XT[:, :, 0:GT], ACT.Copy).then_inc(s["x2_hi"], 1)

            run(sc, step)

        @block.vector
        def _(v):
            for n, (_, _, out) in enumerate(tern):
                v.wait_ge(s["tern_in"], 16 * (n + 1))
                nc.vector.tensor_reduce(abparts[:], stage[:].rearrange("p (a b) -> p a b", a=32), AX_X, ALU.add,
                                        apply_absolute_value=True).then_inc(s["w_abs_parts"], 1)
                v.wait_ge(s["w_abs_parts"], n + 1)
                nc.vector.tensor_reduce(absum[:, n:n + 1], abparts[:], AX_X, ALU.add).then_inc(s["w_abs"], 1)
                v.wait_ge(s["w_alpha_ps"], n + 1)
                nc.vector.tensor_scalar(half_alpha[:, n:n + 1], ps[:, 7, n:n + 1], 0.5 / (D * FF), None,
                                        ALU.mult).then_inc(s["w_alpha"], 1)
                v.wait_ge(s["w_alpha"], n + 1)
                for half in range(2):
                    col = slice(1024 * half, 1024 * half + 1024)
                    k = 2 * n + half
                    wait(v, s["w_sum"], k)
                    nc.vector.tensor_scalar(tern_tmp[:], stage[:, col], -1.0, half_alpha[:, n:n + 1], ALU.mult,
                                            ALU.is_gt).then_inc(s["w_sign"], 1)
                    v.wait_ge(s["w_sign"], k + 1)
                    last = nc.vector.scalar_tensor_tensor(out=out[:, col], in0=stage[:, col],
                                                          scalar=half_alpha[:, n:n + 1], in1=tern_tmp[:],
                                                          op0=ALU.is_gt, op1=ALU.subtract)
                    last.then_inc(s["w_sum"], 1)
            for n, (_, hi_, lo_, cols) in enumerate(chunks):
                v.wait_ge(s["w_hi"], n + 1)
                nc.vector.tensor_tensor(lo_, stage_half[n % 2][:, 0:cols], hi_.bitcast(F32),
                                        ALU.subtract).then_inc(s["w_lo"], 1)
            v.wait_ge(s["qk_ready"], 1)
            nc.vector.scalar_tensor_tensor(out=qk_l[:], in0=SC[:, 0:DC * D].rearrange("p (a b) -> p a b", a=DC),
                                           scalar=float(D) ** -0.5, in1=qk_h[:].bitcast(F32), op0=ALU.mult,
                                           op1=ALU.subtract).then_inc(s["qk_ready"], 1)
            v.wait_ge(s["const_in"], 16)
            v.wait_ge(s["mask_ready"], 1)

            def lo(out, in_, hi_, got, done, g):
                v.wait_ge(got, g + 1)
                nc.vector.tensor_tensor(out, in_, hi_, ALU.subtract).then_inc(done, 1)

            def chunk_parts(g, c):
                k = FC * g + c
                v.wait_ge(s["gelu_done"], k + 1)
                if c == 0:
                    wait(v, s["down_done"], g)
                nc.vector.tensor_copy(act_h[:, c, :], act[:, c % 2, :]).then_inc(s["ffn_hi"], 1)
                if c:
                    v.wait_ge(s["sq_done"], k + 1)
                    if c > 1:
                        v.wait_ge(s["sqsum_done"], (FC - 1) * g + c - 1)
                    nc.vector.tensor_tensor(sqsum[:], sqsum[:], sq[:, c % 2, :], ALU.add).then_inc(s["sqsum_done"], 1)

            def step(g, sl, pr):
                n, m = g + 1, g + 2
                other = 1 - sl
                if has(g, 1):
                    lo(xT_l[:], XT[:, :, 0:GT], xT_h[:].bitcast(F32), s["x_hi"], s["x_lo"], n)
                if has(g, 0):
                    for c in range(4):
                        chunk_parts(g, c)
                if has(g, 1):
                    lo(tT_l[:], ps[:, 2:4, 0:GT], tT_h[:].bitcast(F32), s["t_hi"], s["t_lo"], n)
                    lo(v_l[:], VO[:, 0:TILES * D].rearrange("p (a b) -> p a b", a=TILES), v_h[:].bitcast(F32),
                       s["v_hi"], s["v_lo"], n)
                if has(g, 2):
                    v.wait_ge(s["patch_in"], 16 * (m + 1))
                    wait(v, s["tok_done"], m)
                    nc.vector.tensor_copy(pat_h[:], patches[:]).then_inc(s["patch_hi"], 1)
                if has(g, 0):
                    for c in range(4, FC):
                        chunk_parts(g, c)
                if has(g, 1):
                    v.wait_ge(s["score_done"], n + 1)
                    wait(v, s["pT_done"], n)
                    settle(v)
                    for i in range(TILES):
                        last = nc.vector.tensor_tensor_reduce(prob[:, i, :], SC[:, i * D:(i + 1) * D], mask[:, i, :],
                                                              1.0, MASKED, ALU.add, ALU.max, rowmax[:, i:i + 1])
                    last.then_inc(s["max_done"], 1)
                    v.wait_ge(s["max_done"], n + 1)
                    nc.vector.tensor_scalar(negmax[:], rowmax[:], -1.0, None, ALU.mult).then_inc(s["negmax_done"], 1)
                if has(g, 2):
                    v.wait_ge(s["tok_done"], m + 1)
                    wait(v, s["h1_done"], m - 1)
                    nc.vector.tensor_tensor(emb[:, sl, 0, :], ps[:, 4, 0:D], bias_tok[:], ALU.add).then_inc(s["emb_img"], 1)
                    v.wait_ge(text_in[sl], 32 * (pr + 2))
                    v.wait_ge(s["emb_img"], m + 1)
                    for i in range(TILES):
                        last = nc.vector.bn_stats(stats[:, i, :], emb[:, sl, i, :])
                    last.then_inc(s["ln_stats"], 1)
                    v.wait_ge(s["ln_stats"], m + 1)
                    settle(v)
                    for i in range(TILES):
                        last = nc.vector.bn_aggr(moments[:, i, :], stats[:, i, :])
                    last.then_inc(s["ln_aggr"], 1)
                if has(g, 1):
                    lo(pT_l[:], ps[:, 0:2, :].rearrange("p a b -> p (a b)")[:, 0:5 * P]
                       .rearrange("p (a b) -> p a b", a=5), pT_h[:].bitcast(F32), s["pT_hi"], s["pT_lo"], n)
                    nc.vector.reciprocal(rinv[:], rowsum[:]).then_inc(s["rinv_done"], 1)
                if has(g, 2):
                    v.wait_ge(s["ln_rstd"], m + 1)
                    v.wait_ge(s["ln_aggr"], m + 1)
                    wait(v, s["xT_done"], m)
                    for i in range(TILES):
                        last = nc.vector.tensor_scalar(xn[:, i, :], emb[:, sl, i, :], moments[:, i, 0:1],
                                                       rstd[:, i:i + 1], ALU.subtract, ALU.mult)
                    last.then_inc(s["ln_out"], 1)
                if has(g, 0):
                    v.wait_ge(s["ss_done"], g + 1)
                    nc.vector.tensor_scalar(ms[:], ps[:, 7, D:D + TILES], 1.0 / FF, None, ALU.mult).then_inc(s["ms_done"], 1)
                if has(g, 1):
                    v.wait_ge(s["pv_done"], n + 1)
                    v.wait_ge(s["rinv_done"], n + 1)
                    wait(v, s["stored"], 64 * (n - 1))
                    for i in range(TILES):
                        last = nc.vector.scalar_tensor_tensor(out=h[:, other, i, :], in0=VO[:, i * D:(i + 1) * D],
                                                              scalar=rinv[:, i:i + 1], in1=emb[:, other, i, :],
                                                              op0=ALU.mult, op1=ALU.add)
                    last.then_inc(s["h1_done"], 1)
                    v.wait_ge(s["h1_done"], n + 1)
                    for i in range(TILES):
                        last = nc.vector.bn_stats(stats2[:, i, :], h[:, other, i, :])
                    last.then_inc(s["ln2_stats"], 1)
                    v.wait_ge(s["ln2_stats"], n + 1)
                    settle(v)
                    for i in range(TILES):
                        last = nc.vector.bn_aggr(moments2[:, i, :], stats2[:, i, :])
                    last.then_inc(s["ln2_aggr"], 1)
                if has(g, 0):
                    v.wait_ge(s["rms_done"], g + 1)
                    nc.vector.tensor_scalar(rden[:], rms[:], RMS_EPS, None, ALU.add).then_inc(s["rden_done"], 1)
                    v.wait_ge(s["rden_done"], g + 1)
                    nc.vector.reciprocal(rscale[:], rden[:]).then_inc(s["rscale_done"], 1)
                if has(g, 1):
                    v.wait_ge(s["ln2_roots"], n + 1)
                    nc.vector.scalar_tensor_tensor(out=den2[:], in0=roots[:, 1, :], scalar=RMS_EPS, in1=roots[:, 0, :],
                                                   op0=ALU.mult, op1=ALU.add).then_inc(s["ln2_den"], 1)
                    v.wait_ge(s["ln2_den"], n + 1)
                    nc.vector.reciprocal(scale2[:], den2[:]).then_inc(s["ln2_scale"], 1)
                    v.wait_ge(s["ln2_scale"], n + 1)
                    wait(v, s["x2T_done"], n)
                    for i in range(TILES):
                        last = nc.vector.tensor_scalar(xn2[:, i, :], h[:, other, i, :], moments2[:, i, 0:1],
                                                       scale2[:, i:i + 1], ALU.subtract, ALU.mult)
                    last.then_inc(s["ln2_out"], 1)
                if has(g, 0):
                    v.wait_ge(s["down_done"], g + 1)
                    v.wait_ge(s["rscale_done"], g + 1)
                    for i in range(TILES):
                        last = nc.vector.scalar_tensor_tensor(out=h[:, sl, i, :],
                                                              in0=ps[:, 6 + i // 2, (i % 2) * D:(i % 2 + 1) * D],
                                                              scalar=rscale[:, i:i + 1], in1=h[:, sl, i, :],
                                                              op0=ALU.mult, op1=ALU.add)
                    last.then_inc(s["h2_done"], 1)
                if has(g, 1):
                    lo(x2_l[:], XT[:, :, 0:GT], x2_h[:].bitcast(F32), s["x2_hi"], s["x2_lo"], n)

            run(v, step)

        @block.tensor
        def _(pe):
            for n in range(2):
                pe.wait_ge(s["w_abs"], n + 1)
                nc.tensor.matmul(ps[:, 7, n:n + 1], ones[:], absum[:, n:n + 1], start=True,
                                 stop=True).then_inc(s["w_alpha_ps"], 1)
            pe.wait_ge(s["qk_in"], 32)
            for m in range(DC):
                for k in range(DC):
                    last = nc.tensor.matmul(SC[:, m * D:(m + 1) * D], wq[:, k, m * P:(m + 1) * P], wk[:, k, :],
                                            start=(k == 0), stop=(k == DC - 1))
            last.then_inc(s["merge_ps"], 1)
            pe.wait_ge(s["w_lo"], n_split)
            pe.wait_ge(s["qk_ready"], 2)

            def product(out, terms):
                for n, (a, b) in enumerate(terms):
                    last = nc.tensor.matmul(out, a, b, start=(n == 0), stop=(n == len(terms) - 1))
                return last

            def three(lh, ll, rh, rl, chunks_):
                return [t for k in chunks_ for t in ((lh(k), rh(k)), (lh(k), rl(k)), (ll(k), rh(k)))]

            def up(g, c):
                k = FC * g + c
                if c < 2:
                    wait(pe, s["h2_done"], g)
                    pe.wait_ge(s["x2_lo"], g + 1)
                else:
                    pe.wait_ge(s["gelu_done"], k - 1)
                w = up_w[:]
                product(ps[:, 6 + c % 2, 0:GT],
                        [(w[:, kk, c * P:(c + 1) * P], x[:, kk, :]) for kk in range(DC) for x in (x2_h, x2_l)]
                        ).then_inc(s["up_done"], 1)

            def down(g, i):
                last = None
                if i < 2:
                    pe.wait_ge(s["gelu_done"], FC * g + 7)
                else:
                    pe.wait_ge(s["ms_done"], g + 1)
                for c in range(FC):
                    if i == 0:
                        pe.wait_ge(s["ffn_lo"], FC * g + c + 1)
                    for x in (act_h, act_l):
                        last = nc.tensor.matmul(ps[:, 6 + i // 2, (i % 2) * D:(i % 2 + 1) * D],
                                                x[:, c, i * P:(i + 1) * P], dn_w[:, c, :],
                                                start=(c == 0 and x is act_h), stop=(c == FC - 1 and x is act_l))
                return last

            def step(g, sl, pr):
                n, m = g + 1, g + 2
                if has(g, 1):
                    pe.wait_ge(s["ln_out"], n + 1)
                    wait(pe, s["x2_lo"], n)
                    for i in range(TILES):
                        for c in range(DC):
                            last = nc.tensor.transpose(XT[:, c, i * P:(i + 1) * P], xn[:, i, c * P:(c + 1) * P], ident[:])
                    last.then_inc(s["xT_done"], 1)
                if has(g, 0):
                    for c in range(4):
                        up(g, c)
                if has(g, 1):
                    pe.wait_ge(s["x_lo"], n + 1)
                    wait(pe, s["max_done"], n)
                    for mm in range(DC):
                        last = product(ps[:, 2 + mm, 0:GT],
                                       three(lambda k: qk_h[:, k, mm * P:(mm + 1) * P],
                                             lambda k: qk_l[:, k, mm * P:(mm + 1) * P],
                                             lambda k: xT_h[:, k, :], lambda k: xT_l[:, k, :], range(DC)))
                    last.then_inc(s["t_done"], 1)
                    wait(pe, s["h1_done"], n)
                    pe.wait_ge(s["emb_img"], n + 1)
                    for i in range(TILES):
                        last = product(VO[:, i * D:(i + 1) * D],
                                       three(lambda k: xT_h[:, k, i * P:(i + 1) * P],
                                             lambda k: xT_l[:, k, i * P:(i + 1) * P],
                                             lambda k: wv_h[:, k, :], lambda k: wv_l[:, k, :], range(DC)))
                    last.then_inc(s["v_done"], 1)
                if has(g, 0):
                    for c in range(4, 6):
                        up(g, c)
                if has(g, 1):
                    pe.wait_ge(s["t_lo"], n + 1)

                    def keys(x, k, i):
                        if i < 2:
                            return x[:, k, 0:2 * P]
                        return x[:, k, :].rearrange("p (t c) -> p t c", t=TILES)[:, 0:3:2, :]

                    for i in range(TILES):
                        last = product(SC[:, i * D:(i + 1) * D],
                                       three(lambda k: tT_h[:, k, i * P:(i + 1) * P],
                                             lambda k: tT_l[:, k, i * P:(i + 1) * P],
                                             lambda k: keys(xT_h, k, i), lambda k: keys(xT_l, k, i), range(DC)))
                    last.then_inc(s["score_done"], 1)
                if has(g, 0):
                    for c in range(6, FC):
                        up(g, c)
                if has(g, 2):
                    pe.wait_ge(s["patch_lo"], m + 1)
                    if has(g, 1):
                        pe.wait_ge(s["v_lo"], m)
                    product(ps[:, 4, 0:D], three(lambda k: pat_h[:, k, :], lambda k: pat_l[:, k, :],
                                                 lambda k: tok_h[:, k, :], lambda k: tok_l[:, k, :],
                                                 range(KPC))).then_inc(s["tok_done"], 1)
                if has(g, 0):
                    down(g, 0)
                if has(g, 1):
                    pe.wait_ge(s["exp_done"], n + 1)
                    pairs = ((0, 0), (1, 0), (1, 1), (2, 0), (2, 1))
                    for k, (i, half) in enumerate(pairs):
                        last = nc.tensor.transpose(ps[:, k // 4, (k % 4) * P:(k % 4 + 1) * P],
                                                   prob[:, i, half * P:(half + 1) * P], ident[:])
                    last.then_inc(s["pT_done"], 1)
                if has(g, 0):
                    pe.wait_ge(s["sqsum_done"], (FC - 1) * (g + 1))
                    pe.wait_ge(s["gelu_done"], FC * g + FC)
                    for i in range(TILES):
                        last = nc.tensor.matmul(ps[:, 7, D + i:D + i + 1], sqsum[:, i * P:(i + 1) * P], ones[:, 0:1],
                                                start=True, stop=True)
                    last.then_inc(s["ss_done"], 1)
                    down(g, 1)
                if has(g, 1):
                    pe.wait_ge(s["pT_lo"], n + 1)
                    pe.wait_ge(s["v_lo"], n + 1)
                    if has(g, 2):
                        pe.wait_ge(s["emb_img"], n + 2)
                    terms = (((0, 0),), ((1, 0), (2, 1)), ((3, 0), (4, 2)))
                    for i in range(TILES):
                        last = product(VO[:, i * D:(i + 1) * D],
                                       [t for blk, kt in terms[i] for t in (
                                           (pT_h[:, blk, :], v_h[:, kt, :]), (pT_h[:, blk, :], v_l[:, kt, :]),
                                           (pT_l[:, blk, :], v_h[:, kt, :]))])
                    last.then_inc(s["pv_done"], 1)
                if has(g, 0):
                    down(g, 2).then_inc(s["down_done"], 1)
                if has(g, 1):
                    pe.wait_ge(s["ln2_out"], n + 1)
                    for i in range(TILES):
                        for c in range(DC):
                            last = nc.tensor.transpose(XT[:, c, i * P:(i + 1) * P], xn2[:, i, c * P:(c + 1) * P], ident[:])
                    last.then_inc(s["x2T_done"], 1)

            run(pe, step)


def part_b(nc, W, io, consts):
    with ExitStack() as ctx:
        def sb(name, shape, dt=F32):
            return ctx.enter_context(nc.sbuf_tensor(name, shape, dt))

        ident, ones, halfpow = consts.ident, consts.ones, consts.halfpow
        ln_in = sb("B_ln_in", [P, BTILES, D])
        res = sb("B_residual", [P, 2, BTILES, D])
        stats, moments = sb("B_stats", [P, BTILES, 6]), sb("B_moments", [P, BTILES, 2])
        ve, rstd = sb("B_var_eps", [P, BTILES]), sb("B_rstd", [P, BTILES])
        x_h, x_l = sb("B_x_hi", [P, DC, BT], F32R), sb("B_x_lo", [P, DC, BT], F32R)
        xi_h, xi_l = sb("B_xi_hi", [P, IC, BT], F32R), sb("B_xi_lo", [P, IC, BT], F32R)
        drive = sb("B_xi_then_drive", [P, 2, IC, BT])
        lam = sb("B_lam", [P, 2, IC, BT])
        vv_ = sb("B_v", [P, 2, IC, BT])
        refl = sb("B_reflection", [P, 2, IC, BT])
        gate = sb("B_gate", [P, 2, IC, BT])
        tmp = sb("B_tanh", [P, 2, BT])
        vsq = sb("B_v_squared", [P, BT])
        vsum = sb("B_v_squared_sum", [P, BT])
        inv = sb("B_two_over_vv", [P, BT])
        hs = sb("B_states", [P, IC, BT])
        prod, m_, g_, w_ = (sb("B_" + x, [P, IC, NB]) for x in ("prod", "decayed", "driven", "reflected"))
        dots = sb("B_dots", [P, NB])
        ytmp = sb("B_y", [P, IC, P])
        y_h, y_l = sb("B_y_hi", [P, 2, IC, P], F32R), sb("B_y_lo", [P, 2, IC, P], F32R)
        vec = sb("B_channel_vectors", [P, 3, IC])
        sp_ = sb("B_softplus", [P, 8, IC])
        ps = ctx.enter_context(nc.psum_tensor("psB", [P, 8, 512], F32))

        s = {}
        for name in """ln_in res_in0 res_in1 ln_stats ln_aggr ln_ve ln_rstd ln_out xT_done x_hi x_lo win_done l_done vproj_done
                xi_copy xi_hi xi_lo z_tanh z_gate l_tanh lam_done lam_first drive_done v_done vsq_done vsum_done vv_done inv_done
                lv_done refl_done prod_done decay_done driven_done dot_done sum_done w_done h_done y_done y_hi y_lo
                wout_done res_done stored vec_in half_ready c1 c2 c3 c4 c5 c6 c7 h_zero""".split():
            s[name] = ctx.enter_context(nc.semaphore("B_" + name))

        res_in = [s["res_in0"], s["res_in1"]]

        def at(q, r):
            return slice(q * P + r, (q + 1) * P, 4)

        def tile(q):
            return slice(q * P, (q + 1) * P)

        order = """load_ln.0 xi.0 xi.1 vv.0 inv.0 start.0 xi.2 inv.1 inv.2 inv.3 xi.3 late_wout.3 scan.0 late_res.3 load_res.0
                z.0 z.1 z.2 scan.1  z.3 z.4 z.5 gate.0 scan.2  z.6 z.7 gate.1 l.0 scan.3 y.0  l.1 l.2 l.3 gate.2 scan.4
                ysplit.0 l.4 l.5 l.6 gate.3 scan.5  l.7 l.8 l.9 drive.0 scan.6  l.10 wout.0 stats.0 scan.7 y.1
                l.11 l.12 l.13 res.0 drive.1 scan.8  ysplit.1 l.14 l.15 v.0 stats.1 ln.0 scan.9  v.1 v.2 v.3 drive.2 scan.10
                wout.1 v.4 drive.3 scan.11 y.2  v.5 v.6 v.7 res.1 apply.0 scan.12  ysplit.2 apply.1 v.8 v.9 v.10 scan.13
                turn.0 v.11 v.12 vsum.1 scan.14  wout.2 v.13 res.2 turned.0 scan.15 turned.1 y.3  v.14 v.15 vsum.2
                ysplit.3 vsum.3""".split()
        order = [(kind, int(k)) for kind, k in (w.split(".") for w in order)]

        def part_of(kind):
            return {"xi": 1, "z": 1, "gate": 1, "l": 1, "v": 1, "drive": 1, "vsum": 1, "load_res": 1, "late_wout": -1, "late_res": -1,
                    "stats": 2, "ln": 2, "apply": 2, "turn": 2, "turned": 2, "load_ln": 2}.get(kind, 0)

        def run(eng, piece):
            def step(n, sl, half):
                for kind, k in order:
                    off = part_of(kind)
                    if not isinstance(n, int) or 0 <= n + off < BLOCKS:
                        piece(kind.removeprefix("late_"), k, n + off, (sl + off) % 2, half + (sl + off) // 2)

            for n in (-2, -1, 0, 1):
                step(n, n % 2, n // 2)
            with eng.Fori(1, BLOCKS // 2 - 1) as half_:
                step(2 * half_, 0, half_)
                step(2 * half_ + 1, 1, half_)
            for n in (BLOCKS - 2, BLOCKS - 1, BLOCKS):
                step(n, n % 2, n // 2)

        def bank(j):
            return (2, 3, 4, 2, 3, 4, 2, 5, 3, 4, 2, 3, 4, 2, 3, 5)[j]

        block = ctx.enter_context(nc.Block())

        def rows(t, n, q=None):
            if q is None:
                return t[:, bass.ds(n * STEPS, STEPS), :].rearrange("b (q r) d -> q b r d", q=BTILES)
            return t[:, bass.ds(n * STEPS + 4 * q, 4), :]

        @block.sync
        def _(sp):
            sp.dma_start(vec[:], io["vectors"]).then_inc(s["vec_in"], 16)

            def piece(kind, k, n, sl, half):
                if kind == "load_ln":
                    wait(sp, s["xT_done"], n)
                    for q in range(BTILES):
                        sp.dma_start(ln_in[:, q, :], rows(io["h2"], n, q)).then_inc(s["ln_in"], 16)
                if kind == "load_res":
                    wait(sp, s["stored"], 64 * (n - 1))
                    for q in range(BTILES):
                        sp.dma_start(res[:, sl, q, :], rows(io["h2"], n, q)).then_inc(res_in[sl], 16)
                if kind == "res":
                    sp.wait_ge(s["res_done"], 4 * n + k + 1)
                    sp.dma_start(rows(io["out"], n, k), res[:, sl, k, :]).then_inc(s["stored"], 16)

            run(sp, piece)
            sp.wait_ge(s["stored"], 64 * BLOCKS)

        @block.gpsimd
        def _(pool):
            def piece(kind, k, n, sl, half):
                if kind == "xi":
                    pool.wait_ge(s["xi_hi"], 4 * n + k + 1)
                    nc.gpsimd.tensor_tensor(xi_l[:, k, :], drive[:, sl, k, :], xi_h[:, k, :].bitcast(F32),
                                            ALU.subtract).then_inc(s["xi_lo"], 1)
                if kind == "v" and k % IC == IC - 1:
                    m = k // IC
                    pool.wait_ge(s["v_done"], 4 * n + m + 1)
                    pool.wait_ge(s["lam_done"], 4 * n + m + 1)
                    if isinstance(n, int) and n == 0:
                        pool.wait_ge(s["lam_first"], m + 1)
                    wait(pool, s["h_done"], 16 * (n - 1))
                    nc.gpsimd.tensor_tensor(refl[:, sl, m, :], lam[:, sl, m, :], vv_[:, sl, m, :],
                                            ALU.mult).then_inc(s["lv_done"], 1)
                if kind == "inv":
                    pool.wait_ge(s["inv_done"], 4 * n + k + 1)
                    pool.wait_ge(s["lv_done"], 4 * n + 4)
                    part = refl[:, sl, :, tile(k)]
                    nc.gpsimd.tensor_tensor(part, part, inv[:, tile(k)].rearrange("p (o b) -> p o b", o=1)
                                            .to_broadcast([P, IC, P]), ALU.mult).then_inc(s["refl_done"], 1)
                if kind == "y":
                    pool.wait_ge(s["h_done"], 16 * n + 4 * k + 4)
                    pool.wait_ge(s["z_gate"], 4 * n + 4)
                    wait(pool, s["y_lo"], 4 * n + k)
                    nc.gpsimd.tensor_tensor(ytmp[:], gate[:, sl, :, tile(k)], hs[:, :, tile(k)],
                                            ALU.mult).then_inc(s["y_done"], 1)
                if kind == "ysplit":
                    pool.wait_ge(s["y_hi"], 4 * n + k + 1)
                    nc.gpsimd.tensor_tensor(y_l[:, k % 2, :, :], ytmp[:], y_h[:, k % 2, :, :].bitcast(F32),
                                            ALU.subtract).then_inc(s["y_lo"], 1)
                if kind == "ln":
                    pool.wait_ge(s["ln_aggr"], n + 1)
                    settle(pool)
                    nc.gpsimd.tensor_scalar(ve[:], moments[:, :, 1], LN_EPS, None, ALU.add).then_inc(s["ln_ve"], 1)
                    pool.wait_ge(s["ln_ve"], n + 1)
                    wait(pool, s["ln_out"], 2 * n)
                    nc.gpsimd.tensor_tensor(rstd[:], ve[:], halfpow[:, 1, 0:BTILES], ALU.pow).then_inc(s["ln_rstd"], 1)

            run(pool, piece)

        @block.scalar
        def _(sc):
            sc.wait_ge(s["c1"], 1)
            nc.scalar.activation(sp_[:, 1, :], sp_[:, 0, :], ACT.Exp, scale=-1.0).then_inc(s["c2"], 1)
            sc.wait_ge(s["c3"], 1)
            nc.scalar.activation(sp_[:, 3, :], sp_[:, 2, :], ACT.Ln).then_inc(s["c4"], 1)
            sc.wait_ge(s["half_ready"], 2)

            def piece(kind, k, n, sl, half):
                if kind == "xi":
                    sc.wait_ge(s["win_done"], 8 * n + k + 1)
                    wait(sc, s["h_done"], 16 * (n - 1))
                    nc.scalar.activation(drive[:, sl, k, :], ps[:, bank(k), :], ACT.Copy).then_inc(s["xi_copy"], 1)
                    wait(sc, s["vproj_done"], 4 * n)
                    nc.scalar.activation(xi_h[:, k, :], ps[:, bank(k), :], ACT.Copy).then_inc(s["xi_hi"], 1)
                if kind == "z" and k % DC == DC - 1:
                    m = k // DC
                    sc.wait_ge(s["win_done"], 8 * n + 4 + m + 1)
                    wait(sc, s["z_gate"], 4 * n + m - 1)
                    if m < 2:
                        wait(sc, s["lam_done"], 4 * n)
                    nc.scalar.activation(tmp[:, m % 2, :], ps[:, bank(4 + m), :], ACT.Tanh,
                                         scale=0.5).then_inc(s["z_tanh"], 1)
                if kind == "l" and k % IC == IC - 1:
                    m = k // IC
                    sc.wait_ge(s["l_done"], 4 * n + m + 1)
                    if m < 2:
                        sc.wait_ge(s["z_gate"], 4 * n + 3 + m)
                    else:
                        sc.wait_ge(s["lam_done"], 4 * n + m - 1)
                    nc.scalar.activation(tmp[:, m % 2, :], ps[:, bank(8 + m), :], ACT.Tanh, scale=0.5,
                                         bias=vec[:, 1, m:m + 1]).then_inc(s["l_tanh"], 1)
                    sc.wait_ge(s["l_tanh"], 4 * n + m + 1)
                    wait(sc, s["h_done"], 16 * (n - 1))
                    nc.scalar.activation(lam[:, sl, m, :], tmp[:, m % 2, :], ACT.Exp, scale=sp_[:, 7, m:m + 1],
                                         bias=sp_[:, 7, m:m + 1]).then_inc(s["lam_done"], 1)
                if kind == "v" and k % IC == IC - 1:
                    m = k // IC
                    sc.wait_ge(s["vproj_done"], 4 * n + m + 1)
                    if m == 0:
                        wait(sc, s["vv_done"], n)
                        out = vsum
                    else:
                        wait(sc, s["vsum_done"], 3 * n + m - 1)
                        out = vsq
                    nc.scalar.activation(out[:], ps[:, bank(12 + m), :], ACT.Square,
                                         bias=vec[:, 2, m:m + 1]).then_inc(s["vsq_done"], 1)
                    nc.scalar.activation(vv_[:, sl, m, :], ps[:, bank(12 + m), :], ACT.Identity,
                                         bias=vec[:, 2, m:m + 1]).then_inc(s["v_done"], 1)
                if kind == "ysplit":
                    sc.wait_ge(s["y_done"], 4 * n + k + 1)
                    wait(sc, s["wout_done"], 4 * n + k - 1)
                    nc.scalar.activation(y_h[:, k % 2, :, :], ytmp[:], ACT.Copy).then_inc(s["y_hi"], 1)
                if kind == "turned":
                    sc.wait_ge(s["xT_done"], n + 1)
                    wait(sc, s["win_done"], 8 * n)
                    nc.scalar.activation(x_h[:, k, :], ps[:, k, :], ACT.Copy).then_inc(s["x_hi"], 1)

            run(sc, piece)

        @block.vector
        def _(v):
            v.wait_ge(s["vec_in"], 16)
            omega = vec[:, 0, :]
            nc.vector.scalar_tensor_tensor(out=sp_[:, 0, :], in0=omega, scalar=-1.0, in1=omega, op0=ALU.mult,
                                           op1=ALU.max).then_inc(s["c1"], 1)
            nc.vector.tensor_scalar(vec[:, 1, :], vec[:, 1, :], 0.5, None, ALU.mult).then_inc(s["half_ready"], 1)
            nc.vector.memset(hs[:], 0.0).then_inc(s["h_zero"], 1)
            v.wait_ge(s["c2"], 1)
            nc.vector.tensor_scalar(sp_[:, 2, :], sp_[:, 1, :], 1.0, None, ALU.add).then_inc(s["c3"], 1)
            v.wait_ge(s["c3"], 1)
            v.wait_ge(s["c4"], 1)
            nc.vector.tensor_scalar(sp_[:, 4, :], sp_[:, 2, :], -1.0, None, ALU.add).then_inc(s["c5"], 1)
            v.wait_ge(s["c5"], 1)
            nc.vector.tensor_scalar(sp_[:, 5, :], sp_[:, 4, :], 0.0, None, ALU.is_equal).then_inc(s["c5"], 1)
            v.wait_ge(s["c5"], 2)
            nc.vector.tensor_tensor(sp_[:, 4, :], sp_[:, 4, :], sp_[:, 5, :], ALU.add).then_inc(s["c5"], 1)
            nc.vector.tensor_tensor(sp_[:, 3, :], sp_[:, 3, :], sp_[:, 5, :], ALU.add).then_inc(s["c5"], 1)
            v.wait_ge(s["c5"], 4)
            nc.vector.reciprocal(sp_[:, 6, :], sp_[:, 4, :]).then_inc(s["c6"], 1)
            nc.vector.tensor_tensor(sp_[:, 2, :], sp_[:, 1, :], sp_[:, 3, :], ALU.mult).then_inc(s["c6"], 1)
            v.wait_ge(s["c6"], 2)
            nc.vector.tensor_tensor(sp_[:, 0, :], sp_[:, 2, :], sp_[:, 6, :], ALU.mult).then_inc(s["c7"], 1)
            v.wait_ge(s["c7"], 1)
            nc.vector.scalar_tensor_tensor(out=sp_[:, 1, :], in0=omega, scalar=0.0, in1=sp_[:, 0, :], op0=ALU.max,
                                           op1=ALU.add).then_inc(s["c7"], 1)
            v.wait_ge(s["c7"], 2)
            nc.vector.tensor_scalar(sp_[:, 7, :], sp_[:, 1, :], -C_DECAY / 2, None, ALU.mult).then_inc(s["half_ready"], 1)
            v.wait_ge(s["h_zero"], 1)

            def col(buf, t):
                return buf[:, :, at(t // 4, t % 4)]

            def ahead(n, sl, t):
                prev = col(hs, (t - 1) % STEPS)
                wait(v, s["h_done"], 16 * n + t)
                nc.vector.tensor_tensor(prod[:], col(vv_[:, sl], t), prev, ALU.mult).then_inc(s["prod_done"], 1)
                nc.vector.tensor_tensor(m_[:], col(lam[:, sl], t), prev, ALU.mult).then_inc(s["decay_done"], 1)

            def piece(kind, k, n, sl, half):
                if kind == "gate":
                    v.wait_ge(s["z_tanh"], 4 * n + k + 1)
                    wait(v, s["y_done"], 4 * (n - 1))
                    nc.vector.scalar_tensor_tensor(out=gate[:, sl, k, :], in0=tmp[:, k % 2, :], scalar=1.0,
                                                   in1=ps[:, bank(4 + k), :], op0=ALU.add,
                                                   op1=ALU.mult).then_inc(s["z_gate"], 1)
                if kind == "drive":
                    v.wait_ge(s["lam_done"], 4 * n + k + 1)
                    if isinstance(n, int) and n == 0:
                        nc.vector.memset(lam[:, sl, k, at(0, 0)], 0.0).then_inc(s["lam_first"], 1)
                        v.wait_ge(s["lam_first"], k + 1)
                    v.wait_ge(s["xi_lo"], 4 * n + k + 1)
                    last = nc.vector.scalar_tensor_tensor(out=drive[:, sl, k, :], in0=lam[:, sl, k, :], scalar=1.0,
                                                          in1=drive[:, sl, k, :], op0=ALU.subtract, op1=ALU.mult)
                    last.then_inc(s["drive_done"], 1)
                if kind == "vsum":
                    v.wait_ge(s["vsq_done"], 4 * n + k + 1)
                    wait(v, s["vsum_done"], 3 * n + k - 1)
                    nc.vector.tensor_tensor(vsum[:], vsum[:], vsq[:], ALU.add).then_inc(s["vsum_done"], 1)
                if kind == "inv":
                    v.wait_ge(s["vv_done"], n + 1)
                    wait(v, s["refl_done"], 4 * (n - 1) + k + 1)
                    nc.vector.reciprocal(inv[:, tile(k)], ps[:, 5, tile(k)]).then_inc(s["inv_done"], 1)
                if kind == "start":
                    v.wait_ge(s["v_done"], 4 * n + 4)
                    v.wait_ge(s["drive_done"], 4 * n + 4)
                    ahead(n, sl, 0)
                if kind == "scan":
                    v.wait_ge(s["dot_done"], 16 * n + k + 1)
                    nc.vector.tensor_reduce(dots[:], ps[:, 7, 0:IC * NB].rearrange("p (g b) -> p b g", g=IC), AX_X,
                                            ALU.add).then_inc(s["sum_done"], 1)
                    v.wait_ge(s["decay_done"], 16 * n + k + 1)
                    nc.vector.tensor_tensor(g_[:], m_[:], col(drive[:, sl], k), ALU.subtract).then_inc(s["driven_done"], 1)
                    v.wait_ge(s["sum_done"], 16 * n + k + 1)
                    if k % 4 == 0:
                        v.wait_ge(s["refl_done"], 4 * n + k // 4 + 1)
                        wait(v, s["y_done"], 4 * (n - 1) + k // 4 + 1)
                    nc.vector.tensor_tensor(w_[:], col(refl[:, sl], k),
                                            dots[:].rearrange("p (o b) -> p o b", o=1).to_broadcast([P, IC, NB]),
                                            ALU.mult).then_inc(s["w_done"], 1)
                    v.wait_ge(s["w_done"], 16 * n + k + 1)
                    v.wait_ge(s["driven_done"], 16 * n + k + 1)
                    nc.vector.tensor_tensor(col(hs, k), g_[:], w_[:], ALU.subtract).then_inc(s["h_done"], 1)
                    if k + 1 < STEPS:
                        ahead(n, sl, k + 1)
                if kind == "res":
                    v.wait_ge(s["wout_done"], 4 * n + k + 1)
                    v.wait_ge(res_in[sl], 64 * (half + 1))
                    nc.vector.scalar_tensor_tensor(out=res[:, sl, k, :], in0=ps[:, 6, (k % 2) * D:(k % 2 + 1) * D],
                                                   scalar=0.5, in1=res[:, sl, k, :], op0=ALU.mult,
                                                   op1=ALU.add).then_inc(s["res_done"], 1)
                if kind == "stats":
                    v.wait_ge(s["ln_in"], 64 * (n + 1))
                    for q in (2 * k, 2 * k + 1):
                        last = nc.vector.bn_stats(stats[:, q, :], ln_in[:, q, :])
                    last.then_inc(s["ln_stats"], 1)
                if kind == "ln":
                    v.wait_ge(s["ln_stats"], 2 * n + 2)
                    settle(v)
                    for q in range(BTILES):
                        last = nc.vector.bn_aggr(moments[:, q, :], stats[:, q, :])
                    last.then_inc(s["ln_aggr"], 1)
                if kind == "apply":
                    v.wait_ge(s["ln_rstd"], n + 1)
                    v.wait_ge(s["ln_aggr"], n + 1)
                    for q in (2 * k, 2 * k + 1):
                        last = nc.vector.tensor_scalar(ln_in[:, q, :], ln_in[:, q, :], moments[:, q, 0:1],
                                                       rstd[:, q:q + 1], ALU.subtract, ALU.mult)
                    last.then_inc(s["ln_out"], 1)
                if kind == "turned":
                    v.wait_ge(s["x_hi"], 2 * n + k + 1)
                    nc.vector.tensor_tensor(x_l[:, k, :], ps[:, k, :], x_h[:, k, :].bitcast(F32),
                                            ALU.subtract).then_inc(s["x_lo"], 1)

            run(v, piece)

        @block.tensor
        def _(pe):
            def part(out, lh, ll, rh, rl, ks, first_, last_):
                terms = [t for k in ks for t in ((lh(k), rh(k)), (lh(k), rl(k)), (ll(k), rh(k)))]
                for i, (a, b) in enumerate(terms):
                    last = nc.tensor.matmul(out, a, b, start=(first_ and i == 0), stop=(last_ and i == len(terms) - 1))
                return last

            def win(j, bank_, cs):
                return part(ps[:, bank_, :], lambda c: W.in_h[:, c, j * P:(j + 1) * P],
                            lambda c: W.in_l[:, c, j * P:(j + 1) * P],
                            lambda c: x_h[:, c, :], lambda c: x_l[:, c, :], cs, cs[0] == 0, cs[-1] == DC - 1)

            def project(wh, wl, m, bank_, c):
                return part(ps[:, bank_, :], lambda c: wh[:, c, m * P:(m + 1) * P], lambda c: wl[:, c, m * P:(m + 1) * P],
                            lambda c: xi_h[:, c, :], lambda c: xi_l[:, c, :], [c], c == 0, c == IC - 1)

            def piece(kind, k, n, sl, half):
                if kind == "xi":
                    pe.wait_ge(s["x_lo"], 2 * n + 2)
                    if k < 3:
                        wait(pe, s["v_done"], 4 * (n - 1) + (2, 3, 1)[k])
                    else:
                        pe.wait_ge(s["xi_hi"], 4 * n + 1)
                    win(k, bank(k), [0, 1]).then_inc(s["win_done"], 1)
                if kind == "z":
                    m, c = k // DC, k % DC
                    if c == 0 and m < 3:
                        pe.wait_ge(s["xi_hi"], 4 * n + m + 2)
                    elif c == 0:
                        wait(pe, s["inv_done"], 4 * n)
                    last = win(4 + m, bank(4 + m), [c])
                    if c == DC - 1:
                        last.then_inc(s["win_done"], 1)
                if kind == "l":
                    m, c = k // IC, k % IC
                    if m == 0:
                        pe.wait_ge(s["xi_lo"], 4 * n + c + 1)
                    if c == 0 and m < 3:
                        pe.wait_ge(s["z_gate"], 4 * n + m + 1)
                    elif c == 0:
                        pe.wait_ge(s["l_tanh"], 4 * n + 1)
                    last = project(W.l_h, W.l_l, m, bank(8 + m), c)
                    if c == IC - 1:
                        last.then_inc(s["l_done"], 1)
                if kind == "v":
                    m, c = k // IC, k % IC
                    if c == 0 and m < 3:
                        pe.wait_ge(s["l_tanh"], 4 * n + m + 2)
                    elif c == 0:
                        pe.wait_ge(s["z_gate"], 4 * n + 4)
                    last = project(W.v_h, W.v_l, m, bank(12 + m), c)
                    if c == IC - 1:
                        last.then_inc(s["vproj_done"], 1)
                if kind == "scan":
                    pe.wait_ge(s["prod_done"], 16 * n + k + 1)
                    wait(pe, s["sum_done"], 16 * n + k)
                    nc.tensor.matmul(ps[:, 7, 0:IC * NB], ones[:], prod[:].rearrange("p g b -> p (g b)"), start=True,
                                     stop=True).then_inc(s["dot_done"], 1)
                if kind == "vv":
                    pe.wait_ge(s["vsum_done"], 3 * n + 3)
                    pe.wait_ge(s["v_done"], 4 * n + 4)
                    nc.tensor.matmul(ps[:, 5, :], consts.halves[:], vsum[:], start=True, stop=True).then_inc(s["vv_done"], 1)
                if kind == "wout":
                    pe.wait_ge(s["y_lo"], 4 * n + k + 1)
                    wait(pe, s["res_done"], 4 * n + k)
                    part(ps[:, 6, (k % 2) * D:(k % 2 + 1) * D], lambda c: y_h[:, k % 2, c, :],
                         lambda c: y_l[:, k % 2, c, :], lambda c: W.out_h[:, c, :], lambda c: W.out_l[:, c, :],
                         range(IC), True, True).then_inc(s["wout_done"], 1)
                if kind == "turn":
                    pe.wait_ge(s["ln_out"], 2 * n + 2)
                    wait(pe, s["x_lo"], 2 * n)
                    for q in range(BTILES):
                        for c in range(DC):
                            last = nc.tensor.transpose(ps[:, c, tile(q)], ln_in[:, q, c * P:(c + 1) * P], ident[:])
                    last.then_inc(s["xT_done"], 1)

            run(pe, piece)


def part_c(nc, io, consts):
    MQ = MT // P
    with ExitStack() as ctx:
        def sb(name, shape, dt=F32):
            return ctx.enter_context(nc.sbuf_tensor(name, shape, dt))

        ident, halfpow = consts.ident, consts.halfpow
        acc, xn = sb("C_residual", [P, MQ, D]), sb("C_normed", [P, MQ, D])
        stats, moments = sb("C_stats", [P, MQ, 6]), sb("C_moments", [P, MQ, 2])
        ve, rstd = sb("C_var_eps", [P, MQ]), sb("C_rstd", [P, MQ])
        x_h, x_l = sb("C_x_hi", [P, DC, MT], F32R), sb("C_x_lo", [P, DC, MT], F32R)
        picked, picked_f = sb("C_picked", [P, MQ, 2], I32), sb("C_picked_f", [P, MQ, 2])
        weights = sb("C_routing", [P, MQ, E_N])
        eq = sb("C_is_picked", [P, 2, MQ, E_N])
        wc = sb("C_weight", [P, MQ, E_N])
        wcT = sb("C_weightT", [E_N, MQ, P])
        b_up, b_dn = sb("C_up_bias", [P, E_N, 4]), sb("C_down_bias", [E_N, D])
        raw = sb("C_raw", [P, 2, 6 * D])
        w_h, w_l = sb("C_w_hi", [P, 2, 6 * D], F32R), sb("C_w_lo", [P, 2, 6 * D], F32R)
        gate, up, th, glu = (sb("C_" + x, [P, 2, MT]) for x in ("gate", "up", "tanh", "glu"))
        a_h, a_l = sb("C_act_hi", [P, 2, 2, MT], F32R), sb("C_act_lo", [P, 2, 2, MT], F32R)
        ps = ctx.enter_context(nc.psum_tensor("psC", [P, 8, 512], F32))
        s = {}
        for name in """h_in const_in raw_in0 raw_in1 stats aggr ve rstd normed xT x_hi x_lo cast eq eq_sum wc wcT wcT_copy
                bias bias_added w_hi w_lo gu gate_b up_b up_c tanh glu act a_hi a_lo down acc stored""".split():
            s[name] = ctx.enter_context(nc.semaphore("C_" + name))
        with nc.Block() as clearing:
            @clearing.sync
            def _(sp):
                for sem_ in s.values():
                    sp.sem_clear(sem_)
        raw_in = [s["raw_in0"], s["raw_in1"]]
        rows = io["out"].rearrange("b t d -> (b t) d")[0:MT, :].rearrange("(q p) d -> p q d", p=P)
        block = ctx.enter_context(nc.Block())

        @block.sync
        def _(sp):
            sp.dma_start(acc[:], rows).then_inc(s["h_in"], 16)
            for a, b in ((picked, io["picked"]), (weights, io["routing"]), (b_up, io["up_bias"]), (b_dn, io["down_bias"])):
                sp.dma_start(a[:], b).then_inc(s["const_in"], 16)
            for e in range(E_N):
                if e >= 2:
                    sp.wait_ge(s["w_lo"], e - 1)
                sp.dma_start(raw[:, e % 2, :], io["experts"][e]).then_inc(raw_in[e % 2], 16)
            sp.wait_ge(s["acc"], MQ * E_N)
            sp.dma_start(rows, acc[:]).then_inc(s["stored"], 16)
            sp.wait_ge(s["stored"], 16)

        @block.gpsimd
        def _(pool):
            def split(e):
                pool.wait_ge(s["w_hi"], e + 1)
                nc.gpsimd.tensor_tensor(w_l[:, e % 2, :], raw[:, e % 2, :], w_h[:, e % 2, :].bitcast(F32),
                                        ALU.subtract).then_inc(s["w_lo"], 1)

            split(0)
            pool.wait_ge(s["aggr"], 1)
            nc.gpsimd.tensor_scalar(ve[:], moments[:, :, 1], LN_EPS, None, ALU.add).then_inc(s["ve"], 1)
            pool.wait_ge(s["ve"], 1)
            nc.gpsimd.tensor_tensor(rstd[:], ve[:], halfpow[:, 1, 0:MQ], ALU.pow).then_inc(s["rstd"], 1)
            split(1)
            for e in range(E_N):
                pool.wait_ge(s["a_hi"], e + 1)
                nc.gpsimd.tensor_tensor(a_l[:, e % 2, :, :], glu[:], a_h[:, e % 2, :, :].bitcast(F32),
                                        ALU.subtract).then_inc(s["a_lo"], 1)
                if e + 2 < E_N:
                    split(e + 2)

        @block.scalar
        def _(sc):
            def split(e):
                sc.wait_ge(raw_in[e % 2], 16 * (e // 2 + 1))
                if e >= 2:
                    sc.wait_ge(s["down"], MQ * (e - 1))
                nc.scalar.activation(w_h[:, e % 2, :], raw[:, e % 2, :], ACT.Copy).then_inc(s["w_hi"], 1)

            split(0)
            split(1)
            sc.wait_ge(s["xT"], 1)
            nc.scalar.activation(x_h[:], ps[:, 0:2, :], ACT.Copy).then_inc(s["x_hi"], 1)
            for e in range(E_N):
                for m in range(2):
                    sc.wait_ge(s["gate_b"], 2 * e + m + 1)
                    if e:
                        sc.wait_ge(s["glu"], 2 * (e - 1) + m + 1)
                    nc.scalar.activation(th[:, m, :], gate[:, m, :], ACT.Tanh, scale=ALPHA / 2).then_inc(s["tanh"], 1)
                sc.wait_ge(s["act"], 2 * e + 2)
                if e >= 2:
                    sc.wait_ge(s["down"], MQ * (e - 1))
                nc.scalar.activation(a_h[:, e % 2, :, :], glu[:], ACT.Copy).then_inc(s["a_hi"], 1)
                if e + 2 < E_N:
                    split(e + 2)

        @block.vector
        def _(v):
            v.wait_ge(s["h_in"], 16)
            for q in range(MQ):
                last = nc.vector.bn_stats(stats[:, q, :], acc[:, q, :])
            last.then_inc(s["stats"], 1)
            v.wait_ge(s["stats"], 1)
            for q in range(MQ):
                last = nc.vector.bn_aggr(moments[:, q, :], stats[:, q, :])
            last.then_inc(s["aggr"], 1)
            v.wait_ge(s["const_in"], 64)
            nc.vector.tensor_copy(picked_f[:], picked[:]).then_inc(s["cast"], 1)
            v.wait_ge(s["cast"], 1)
            for k in range(2):
                for e in range(E_N):
                    last = nc.vector.tensor_scalar(eq[:, k, :, e], picked_f[:, :, k], float(e), None, ALU.is_equal)
            last.then_inc(s["eq"], 1)
            v.wait_ge(s["eq"], 1)
            nc.vector.tensor_tensor(wc[:], eq[:, 0], eq[:, 1], ALU.add).then_inc(s["eq_sum"], 1)
            v.wait_ge(s["eq_sum"], 1)
            nc.vector.tensor_tensor(wc[:], wc[:], weights[:], ALU.mult).then_inc(s["wc"], 1)
            v.wait_ge(s["rstd"], 1)
            v.wait_ge(s["aggr"], 1)
            for q in range(MQ):
                last = nc.vector.tensor_scalar(xn[:, q, :], acc[:, q, :], moments[:, q, 0:1], rstd[:, q:q + 1],
                                               ALU.subtract, ALU.mult)
            last.then_inc(s["normed"], 1)
            v.wait_ge(s["x_hi"], 1)
            nc.vector.tensor_tensor(x_l[:], ps[:, 0:2, :], x_h[:].bitcast(F32), ALU.subtract).then_inc(s["x_lo"], 1)
            v.wait_ge(s["wcT"], 1)
            nc.vector.tensor_copy(wcT[:].rearrange("p a b -> p (a b)"), ps[0:E_N, 6, :]).then_inc(s["wcT_copy"], 1)
            v.wait_ge(s["bias"], 1)
            nc.vector.tensor_tensor(acc[:].rearrange("p a b -> p (a b)"), acc[:].rearrange("p a b -> p (a b)"),
                                    ps[:, 0:2, :].rearrange("p a b -> p (a b)"), ALU.add).then_inc(s["bias_added"], 1)
            v.wait_ge(s["bias_added"], 1)
            v.wait_ge(s["wc"], 1)

            def combine(e):
                for q in range(MQ):
                    v.wait_ge(s["down"], MQ * e + q + 1)
                    wait(v, s["acc"], MQ * (e - 1) + q + 1)
                    nc.vector.scalar_tensor_tensor(out=acc[:, q, :], in0=ps[:, (6, 7, 0, 1)[q], 0:D],
                                                   scalar=wc[:, q, e:e + 1], in1=acc[:, q, :], op0=ALU.mult,
                                                   op1=ALU.add).then_inc(s["acc"], 1)

            for e in range(E_N):
                for m in range(2):
                    v.wait_ge(s["gu"], 4 * e + m + 1)
                    if e:
                        v.wait_ge(s["tanh"], 2 * (e - 1) + m + 1)
                        v.wait_ge(s["glu"], 2 * (e - 1) + m + 1)
                    nc.vector.tensor_scalar(gate[:, m, :], ps[:, 2 + m, :], b_up[:, e, m:m + 1], LIMIT, ALU.add,
                                            ALU.min).then_inc(s["gate_b"], 1)
                for m in range(2):
                    v.wait_ge(s["gu"], 4 * e + 2 + m + 1)
                    if e:
                        v.wait_ge(s["act"], 2 * (e - 1) + m + 1)
                    nc.vector.tensor_scalar(up[:, m, :], ps[:, 4 + m, :], b_up[:, e, 2 + m:3 + m], -LIMIT, ALU.add,
                                            ALU.max).then_inc(s["up_b"], 1)
                    v.wait_ge(s["up_b"], 2 * e + m + 1)
                    nc.vector.tensor_scalar(up[:, m, :], up[:, m, :], LIMIT, 1.0, ALU.min,
                                            ALU.add).then_inc(s["up_c"], 1)
                if e:
                    combine(e - 1)
                for m in range(2):
                    v.wait_ge(s["tanh"], 2 * e + m + 1)
                    if e:
                        v.wait_ge(s["a_lo"], e)
                    nc.vector.scalar_tensor_tensor(out=glu[:, m, :], in0=th[:, m, :], scalar=1.0, in1=gate[:, m, :],
                                                   op0=ALU.add, op1=ALU.mult).then_inc(s["glu"], 1)
                    v.wait_ge(s["glu"], 2 * e + m + 1)
                    v.wait_ge(s["up_c"], 2 * e + m + 1)
                    nc.vector.scalar_tensor_tensor(out=glu[:, m, :], in0=glu[:, m, :], scalar=0.5, in1=up[:, m, :],
                                                   op0=ALU.mult, op1=ALU.mult).then_inc(s["act"], 1)
            combine(E_N - 1)

        @block.tensor
        def _(pe):
            def product(out, lh, ll, rh, rl):
                terms = [t for k in range(DC) for t in ((lh(k), rh(k)), (lh(k), rl(k)), (ll(k), rh(k)))]
                for i, (a, b) in enumerate(terms):
                    last = nc.tensor.matmul(out, a, b, start=(i == 0), stop=(i == len(terms) - 1))
                return last

            pe.wait_ge(s["normed"], 1)
            for q in range(MQ):
                for c in range(DC):
                    last = nc.tensor.transpose(ps[:, c, q * P:(q + 1) * P], xn[:, q, c * P:(c + 1) * P], ident[:])
            last.then_inc(s["xT"], 1)
            pe.wait_ge(s["wc"], 1)
            for q in range(MQ):
                last = nc.tensor.transpose(ps[0:E_N, 6, q * P:(q + 1) * P], wc[:, q, :], ident[:])
            last.then_inc(s["wcT"], 1)
            pe.wait_ge(s["x_lo"], 1)
            pe.wait_ge(s["wcT_copy"], 1)
            for q in range(MQ):
                last = nc.tensor.matmul(ps[:, q // 2, (q % 2) * D:(q % 2 + 1) * D], wcT[:, q, :], b_dn[:], start=True,
                                        stop=True)
            last.then_inc(s["bias"], 1)

            def gate_up(e):
                pe.wait_ge(s["w_lo"], e + 1)
                for m in range(4):
                    if e:
                        pe.wait_ge(s["gate_b"] if m < 2 else s["up_b"], 2 * (e - 1) + m % 2 + 1)
                    product(ps[:, 2 + m, :], lambda k: w_h[:, e % 2, k * 2 * D + m * P:k * 2 * D + (m + 1) * P],
                            lambda k: w_l[:, e % 2, k * 2 * D + m * P:k * 2 * D + (m + 1) * P],
                            lambda k: x_h[:, k, :], lambda k: x_l[:, k, :]).then_inc(s["gu"], 1)

            def down(e):
                pe.wait_ge(s["a_lo"], e + 1)
                for q in range(MQ):
                    if e == 0:
                        pe.wait_ge(s["bias_added"], 1)
                    else:
                        pe.wait_ge(s["acc"], MQ * (e - 1) + q + 1)
                    product(ps[:, (6, 7, 0, 1)[q], 0:D], lambda k: a_h[:, e % 2, k, q * P:(q + 1) * P],
                            lambda k: a_l[:, e % 2, k, q * P:(q + 1) * P],
                            lambda k: w_h[:, e % 2, 4 * D + k * D:4 * D + (k + 1) * D],
                            lambda k: w_l[:, e % 2, 4 * D + k * D:4 * D + (k + 1) * D]).then_inc(s["down"], 1)

            gate_up(0)
            for e in range(1, E_N):
                gate_up(e)
                down(e - 1)
            down(E_N - 1)


def program(nc, io):
    with ExitStack() as ctx:
        consts, W = Names(), Names()

        def sb(name, shape, dt=F32):
            return ctx.enter_context(nc.sbuf_tensor(name, shape, dt))

        consts.ident, consts.ones, consts.halves = sb("ident", [P, P]), sb("ones", [P, P]), sb("halves", [P, P])
        consts.halfpow = sb("half_powers", [P, 2, 4])
        W.in_h, W.in_l = sb("Win_hi", [P, DC, 2 * DI], F32R), sb("Win_lo", [P, DC, 2 * DI], F32R)
        W.l_h, W.l_l = sb("Wl_hi", [P, IC, DI], F32R), sb("Wl_lo", [P, IC, DI], F32R)
        W.v_h, W.v_l = sb("Wv_hi", [P, IC, DI], F32R), sb("Wv_lo", [P, IC, DI], F32R)
        W.out_h, W.out_l = sb("Wout_hi", [P, IC, D], F32R), sb("Wout_lo", [P, IC, D], F32R)
        zeroed = ctx.enter_context(nc.semaphore("ident_zeroed"))
        made = ctx.enter_context(nc.semaphore("consts_made"))
        with nc.Block() as block:
            @block.gpsimd
            def _(pool):
                nc.gpsimd.memset(consts.ident[:], 0.0).then_inc(zeroed, 1)
                nc.gpsimd.memset(consts.ones[:], 1.0)
                nc.gpsimd.memset(consts.halves[:], 0.5)
                nc.gpsimd.memset(consts.halfpow[:, 0, :], 0.5)
                nc.gpsimd.memset(consts.halfpow[:, 1, :], -0.5)
                pool.wait_ge(zeroed, 1)
                nc.gpsimd.affine_select(out=consts.ident[:], in_=consts.ident[:], compare_op=ALU.not_equal, fill=1.0,
                                        base=0, pattern=[[-1, P]], channel_multiplier=1).then_inc(made, 1)
                pool.wait_ge(made, 1)
        part_a(nc, W, io, consts)
        part_b(nc, W, io, consts)
        part_c(nc, io, consts)


def kernel(x, x_txt, L0_tok_W, L0_tok_b, L0_txt_weight, L0_attn_wq, L0_attn_wk, L0_attn_wv, L0_ffn_w_up,
           L0_ffn_w_down, L1_attn_omega, L1_attn_Win, L1_attn_Wl, L1_attn_bl, L1_attn_Wv, L1_attn_bv, L1_attn_Wout,
           L1_ffn_router_indices, L1_ffn_routing_weights, L1_ffn_gate_up_proj, L1_ffn_gate_up_proj_bias,
           L1_ffn_down_proj, L1_ffn_down_proj_bias):
    import numpy as np
    import concourse.bacc as bacc
    from concourse.bass_utils import run_bass_kernel_spmd as run

    def rows(a):
        a = np.asarray(a)
        c = a.shape[0] // P
        return a.reshape(c, P, -1).transpose(1, 0, 2).reshape(P, -1)

    x = np.asarray(x)
    pat = x.reshape(G, 2, 3, 8, 16, 8, 16).transpose(0, 2, 4, 6, 1, 3, 5).reshape(G, KPC, P, P).transpose(0, 2, 1, 3)
    vectors = np.stack([np.asarray(a).reshape(IC, P).T for a in (L1_attn_omega, L1_attn_bl, L1_attn_bv)], axis=1)
    gu = np.asarray(L1_ffn_gate_up_proj)
    gu = np.concatenate([gu[..., 0::2], gu[..., 1::2]], axis=-1)
    gub = np.asarray(L1_ffn_gate_up_proj_bias)
    gub = np.concatenate([gub[..., 0::2], gub[..., 1::2]], axis=-1)
    dn = np.asarray(L1_ffn_down_proj)
    experts = np.concatenate([np.stack([rows(gu[e]) for e in range(E_N)]),
                              np.stack([rows(dn[e]) for e in range(E_N)])], axis=-1)
    arrays = {
        "patches": pat, "ids": np.asarray(x_txt).reshape(G, 2, P).transpose(0, 2, 1),
        "tokW": rows(L0_tok_W), "tokb": np.broadcast_to(np.asarray(L0_tok_b), (P, D)), "table": L0_txt_weight,
        "wq": rows(L0_attn_wq), "wk": rows(L0_attn_wk), "wvT": rows(np.asarray(L0_attn_wv).T),
        "upT": rows(np.asarray(L0_ffn_w_up).T), "downT": rows(np.asarray(L0_ffn_w_down).T),
        "vectors": vectors, "WinT": rows(np.asarray(L1_attn_Win).T), "WlT": rows(np.asarray(L1_attn_Wl).T),
        "WvT": rows(np.asarray(L1_attn_Wv).T), "WoutT": rows(np.asarray(L1_attn_Wout).T),
        "picked": np.asarray(L1_ffn_router_indices).reshape(MT // P, P, 2).transpose(1, 0, 2),
        "routing": np.asarray(L1_ffn_routing_weights).reshape(MT // P, P, E_N).transpose(1, 0, 2),
        "up_bias": gub.reshape(E_N, 4, P).transpose(2, 0, 1), "down_bias": L1_ffn_down_proj_bias,
        "experts": experts,
    }
    nc = bacc.Bacc("TRN2", target_bir_lowering=False, num_devices=1)
    io, ins = {}, {}
    for name, a in arrays.items():
        a = np.ascontiguousarray(np.asarray(a))
        ins[f"in_{name}"] = a
        io[name] = nc.dram_tensor(f"in_{name}", a.shape, mybir.dt.from_np(a.dtype), kind="ExternalInput").ap()
    io["wq"] = io["wq"].rearrange("p (k n) -> p k n", k=DC)
    io["wk"] = io["wk"].rearrange("p (k n) -> p k n", k=DC)
    io["h2"] = nc.dram_tensor("layer0_out", (NB, T, D), F32, kind="Internal").ap()
    io["out"] = nc.dram_tensor("out_dram", (NB, T, D), F32, kind="ExternalOutput").ap()
    program(nc, io)
    r = run(nc, [ins], core_ids=[0])
    return r.results[0]["out_dram"]
```

```python
from contextlib import ExitStack

import concourse.bass as bass
from concourse import mybir

ALU = mybir.AluOpType
ACT = mybir.ActivationFunctionType
F32 = mybir.dt.float32
F32R = mybir.dt.float32r
I32 = mybir.dt.int32
U32 = mybir.dt.uint32
AX_X = mybir.AxisListType.X

P = 128
NB = 32
D = 256
DC = D // P
N_IMG = 64
N_TXT = 128
T = N_IMG + N_TXT
KP = 3 * 16 * 16
KPC = KP // P
FF = 1024
FC = FF // P
G = NB // 2
TILES = 3
GT = TILES * P
DI = 512
IC = DI // P
STEPS = 16
BLOCKS = T // STEPS
BT = STEPS * NB
BTILES = BT // P
C_DECAY = 8.0
LN_EPS = 1e-5
RMS_EPS = 1e-8
MASKED = -3.0e38
E_N = 8
MT = 512
LIMIT = 7.0
ALPHA = 1.702


def wait(eng, sem, count):
    if isinstance(count, int) and count <= 0:
        return
    eng.wait_ge(sem, count)


def settle(eng):
    eng.nop(nofuse=True)


class Names:
    pass


DEEP = 4


def part_a(nc, W, io, consts):
    with ExitStack() as ctx:
        def sb(name, shape, dt=F32):
            return ctx.enter_context(nc.sbuf_tensor(name, shape, dt))

        def sem(name):
            return ctx.enter_context(nc.semaphore(name))

        stage = sb("weight_stage", [P, 4 * DI])
        absum, abparts = sb("abs_sum", [P, 4]), sb("abs_sum_parts", [P, 32])
        half_alpha = sb("half_alpha", [P, 2])
        bias_tok = sb("patch_bias", [P, D])
        ids = sb("text_ids", [P, 2, 2], I32)
        tok_h, tok_l = sb("tokW_hi", [P, KPC, D], F32R), sb("tokW_lo", [P, KPC, D], F32R)
        qk_h, qk_l = sb("qk_hi", [P, DC, D], F32R), sb("qk_lo", [P, DC, D], F32R)
        wv_h, wv_l = sb("wv_hi", [P, DC, D], F32R), sb("wv_lo", [P, DC, D], F32R)
        up_w = sb("ternary_up", [P, DC, FF], F32R)
        dn_w = sb("ternary_down", [P, FC, D], F32R)
        mask = sb("causal_mask", [P, TILES, D])
        patches = sb("patches", [P, KPC, P])
        pat_h, pat_l = sb("patches_hi", [P, KPC, P], F32R), sb("patches_lo", [P, KPC, P], F32R)
        emb = sb("embedded", [P, 2, TILES, D])
        stats, moments = sb("ln_stats", [P, TILES, 6]), sb("ln_moments", [P, TILES, 2])
        ve, rstd = sb("ln_var_eps", [P, TILES]), sb("ln_rstd", [P, TILES])
        xn = sb("x_normed", [P, TILES, D])
        xT_h, xT_l = sb("xT_hi", [P, DC, GT], F32R), sb("xT_lo", [P, DC, GT], F32R)
        tT_h, tT_l = sb("tT_hi", [P, DC, GT], F32R), sb("tT_lo", [P, DC, GT], F32R)
        v_h, v_l = sb("v_hi", [P, TILES, D], F32R), sb("v_lo", [P, TILES, D], F32R)
        prob = sb("probs", [P, TILES, D])
        rowmax, negmax = sb("row_max", [P, TILES]), sb("neg_max", [P, TILES])
        rowsum, rinv = sb("row_sum", [P, TILES]), sb("row_inv", [P, TILES])
        pT_h, pT_l = sb("probT_hi", [P, 5, P], F32R), sb("probT_lo", [P, 5, P], F32R)
        h = sb("residual", [P, 2, TILES, D])
        stats2, moments2 = sb("ln2_stats", [P, TILES, 6]), sb("ln2_moments", [P, TILES, 2])
        pair, roots = sb("ln2_pair", [P, 2, TILES]), sb("ln2_roots", [P, 2, TILES])
        den2, scale2 = sb("ln2_den", [P, TILES]), sb("ln2_scale", [P, TILES])
        xn2 = sb("x2_normed", [P, TILES, D])
        x2_h, x2_l = sb("x2T_hi", [P, DC, GT], F32R), sb("x2T_lo", [P, DC, GT], F32R)
        act = sb("gelu_out", [P, DEEP, GT])
        sq = sb("gelu_sq", [P, DEEP, GT])
        warm = sb("exp_table_warm", [P, 1])
        sqsum = sb("gelu_sq_sum", [P, GT])
        act_h, act_l = sb("gelu_hi", [P, FC, GT], F32R), sb("gelu_lo", [P, FC, GT], F32R)
        flat_act = act[:].rearrange("p a b -> p (a b)")
        wq, wk = (flat_act[:, i * DC * D:(i + 1) * DC * D].rearrange("p (a b) -> p a b", a=DC) for i in range(2))
        tern_tmp = sq[:].rearrange("p a b -> p (a b)")[:, 0:1024]
        ms, rms = sb("rms_mean", [P, TILES]), sb("rms_root", [P, TILES])
        rden, rscale = sb("rms_den", [P, TILES]), sb("rms_scale", [P, TILES])
        ps = ctx.enter_context(nc.psum_tensor("psA", [P, 8, 512], F32))
        XT = ps[:, 0:2, :]
        SC = ps[:, 2:4, :].rearrange("p a b -> p (a b)")
        VO = ps[:, 4:6, :].rearrange("p a b -> p (a b)")
        ident, ones, halfpow = consts.ident, consts.ones, consts.halfpow

        s = {}
        for name in """tern_in stage_in0 stage_in1 ids_in0 ids_in1 w_hi w_lo w_abs_parts w_abs w_alpha w_alpha_ps w_sum w_sign const_in mask_zero mask_ready
                merge_ps qk_in qk_ready
                patch_in patch_hi patch_lo tok_done emb_img text_in0 text_in1 ln_stats ln_aggr ln_ve ln_rstd ln_out xT_done
                x_hi x_lo t_done t_hi t_lo v_done v_hi v_lo score_done max_done negmax_done exp_done pT_done pT_hi
                pT_lo pv_done rinv_done h1_done ln2_stats ln2_aggr ln2_pair ln2_roots ln2_den ln2_scale ln2_out
                x2T_done x2_hi x2_lo up_done gelu_done sq_done ffn_hi ffn_lo ffn_lo_v sqsum_done ss_done ms_done rms_done
                warmed rden_done rscale_done down_done h2_done stored""".split():
            s[name] = sem("A_" + name)

        def flat(t):
            return t[:].rearrange("p a b -> p (a b)")

        chunks = []
        for src, hi, lo in ((io["tokW"], tok_h, tok_l), (io["wvT"], wv_h, wv_l), (io["WinT"], W.in_h, W.in_l),
                            (io["WlT"], W.l_h, W.l_l), (io["WvT"], W.v_h, W.v_l), (io["WoutT"], W.out_h, W.out_l)):
            cols = flat(hi).shape[1]
            for a in range(0, cols, 1024):
                b = min(cols, a + 1024)
                chunks.append((src[:, a:b], flat(hi)[:, a:b], flat(lo)[:, a:b], b - a))
        tern = [(io["upT"], 0, flat(up_w)), (io["downT"], 1, flat(dn_w))]

        block = ctx.enter_context(nc.Block())

        order = """ids_load exp tok ternary.0 up.0 up.1 pT patch_split patch_load emb pT_split root1 gelu.0 v v_split
                gelu.1 up.2 up.3 gelu.2 add.1 apply1 pv up.4 gelu.3 add.2 xT gelu.4 up.5 x_split ternary.1 gelu.5 up.6
                add.3 up.7 gelu.6 gelu.7 exp_table t h1 root2 gather t_split add.4 add.5 down.0 down.1 score
                scale2 add.6 add.7 x2T ss down.2 max x2_split rscale h2.0 h2.1 h2.2""".split()
        order = [(w.split(".")[0], int((w + ".0").split(".")[1])) for w in order]
        offset = {"up": 0, "gelu": 0, "add": 0, "down": 0, "ss": 0, "rscale": 0, "h2": 0, "tok": 2, "emb": 2, "root1": 2, "apply1": 2,
                  "xT": 2, "x_split": 2, "t": 2, "t_split": 2, "score": 2, "max": 2, "ternary": 2, "patch_load": 4, "ids_load": 3,
                  "patch_split": 3, "gather": 3}

        def run(eng, piece, prepare=None):
            def step(g, sl, half):
                if prepare is not None and isinstance(g, int):
                    prepare(g)
                for kind, k in order:
                    off = offset.get(kind, 1)
                    if not isinstance(g, int) or 0 <= g + off < G:
                        piece(kind, k, g + off, (sl + off) % 2, half + (sl + off) // 2)

            for g in (-4, -3, -2, -1, 0, 1):
                step(g, g % 2, g // 2)
            with eng.Fori(1, G // 2 - 2) as half_:
                step(2 * half_, 0, half_)
                step(2 * half_ + 1, 1, half_)
            for g in range(G - 4, G):
                step(g, g % 2, g // 2)

        chunks_of = {-3: (0, 1, 2), 0: (3, 4), 1: (5, 6), G - 4: (7, 8), G - 3: (9,)}
        tern_of = {-2: (0, 1)}

        def existing(n):
            return min(n + 1, G) if isinstance(n, int) else n + 1

        lo_vector = (3, 5, 7)
        lo_pool = [k for k in range(FC) if k not in lo_vector]

        def wait_lo(eng, n, k):
            if k < 0:
                n, k = n - 1, k + FC
            if isinstance(n, int) and n < 0:
                return
            if k in lo_vector:
                eng.wait_ge(s["ffn_lo_v"], len(lo_vector) * n + lo_vector.index(k) + 1)
            else:
                eng.wait_ge(s["ffn_lo"], len(lo_pool) * n + lo_pool.index(k) + 1)

        stage_in = [s["stage_in0"], s["stage_in1"]]
        text_in = [s["text_in0"], s["text_in1"]]
        ids_in = [s["ids_in0"], s["ids_in1"]]
        stage_half = [stage[:, 0:1024], stage[:, 1024:2048]]

        @block.sync
        def _(sp):
            def prepare(g):
                for n in chunks_of.get(g, ()):
                    src, _, _, cols = chunks[n]
                    if n >= 2:
                        sp.wait_ge(s["w_lo"], n - 1)
                    if n in (3, 4):
                        sp.wait_ge(s["w_sum"], 4)
                    sp.dma_start(stage_half[n % 2][:, 0:cols], src).then_inc(stage_in[n % 2], 16)
                if g == -3:
                    sp.dma_start(wq, io["wq"]).then_inc(s["qk_in"], 16)
                    sp.dma_start(wk, io["wk"]).then_inc(s["qk_in"], 16)
                    sp.dma_start(bias_tok[:], io["tokb"]).then_inc(s["const_in"], 16)
                for n in tern_of.get(g, ()):
                    sp.wait_ge(s["w_lo"], 3)
                    wait(sp, s["w_sum"], 2 * n)
                    sp.dma_start(stage[:], tern[n][0]).then_inc(s["tern_in"], 16)

            def piece(kind, k, n, sl, half):
                if kind == "patch_load":
                    wait(sp, s["patch_lo"], n)
                    wait(sp, s["patch_hi"], n)
                    sp.dma_start(patches[:], io["patches"][n]).then_inc(s["patch_in"], 16)
                if kind == "ids_load":
                    wait(sp, text_in[sl], 32 * half)
                    sp.dma_start(ids[:, sl, :], io["ids"][n]).then_inc(ids_in[sl], 16)
                if kind == "h2" and k == TILES - 1:
                    sp.wait_ge(s["h2_done"], TILES * (n + 1))
                    for j in range(2):
                        sp.dma_start(io["h2"][2 * n + j, 0:N_IMG, :],
                                     h[j * N_IMG:(j + 1) * N_IMG, sl, 0, :]).then_inc(s["stored"], 16)
                        sp.dma_start(io["h2"][2 * n + j, N_IMG:T, :], h[:, sl, 1 + j, :]).then_inc(s["stored"], 16)

            run(sp, piece, prepare)
            sp.wait_ge(s["stored"], 64 * G)

        @block.gpsimd
        def _(pool):
            nc.gpsimd.memset(mask[:], 0.0).then_inc(s["mask_zero"], 1)
            pool.wait_ge(s["mask_zero"], 1)
            nc.gpsimd.affine_select(out=mask[:, 0, :], in_=mask[:, 0, :], compare_op=ALU.is_ge, fill=MASKED,
                                    base=0, pattern=[[-1, D]], channel_multiplier=1).then_inc(s["mask_zero"], 1)
            pool.wait_ge(s["mask_zero"], 2)
            nc.gpsimd.affine_select(out=mask[:, 0, 0:N_IMG], in_=mask[:, 0, 0:N_IMG], compare_op=ALU.is_ge,
                                    fill=MASKED, base=N_IMG - 1, pattern=[[0, N_IMG]],
                                    channel_multiplier=-1).then_inc(s["mask_zero"], 1)
            nc.gpsimd.memset(mask[:, 1, N_IMG:2 * N_IMG], MASKED)
            nc.gpsimd.memset(mask[:, 2, 0:N_IMG], MASKED)
            nc.gpsimd.affine_select(out=mask[:, 1:3, P:2 * P], in_=mask[:, 1:3, P:2 * P], compare_op=ALU.is_ge,
                                    fill=MASKED, base=0, pattern=[[0, 2], [-1, P]],
                                    channel_multiplier=1).then_inc(s["mask_ready"], 1)

            def piece(kind, k, n, sl, half):
                if kind == "gather":
                    pool.wait_ge(ids_in[sl], 16 * (half + 1))
                    wait(pool, s["h1_done"], n - 1)
                    settle(pool)
                    for j in range(2):
                        pool.indirect_dma_start(
                            emb[:, sl, 1 + j, :], None, io["table"],
                            bass.IndirectOffsetOnAxis(ap=ids[:, sl, j:j + 1], axis=0),
                        ).then_inc(text_in[sl], 16)
                if kind == "gelu" and k in lo_pool:
                    pool.wait_ge(s["ffn_hi"], FC * n + k + 1)
                    nc.gpsimd.tensor_tensor(act_l[:, k, :], act[:, k % DEEP, :], act_h[:, k, :].bitcast(F32),
                                            ALU.subtract).then_inc(s["ffn_lo"], 1)
                if kind == "patch_split":
                    pool.wait_ge(s["patch_hi"], n + 1)
                    nc.gpsimd.tensor_tensor(pat_l[:], patches[:], pat_h[:].bitcast(F32),
                                            ALU.subtract).then_inc(s["patch_lo"], 1)
                if kind == "root1":
                    pool.wait_ge(s["ln_aggr"], n + 1)
                    settle(pool)
                    nc.gpsimd.tensor_scalar(ve[:], moments[:, :, 1], LN_EPS, None, ALU.add).then_inc(s["ln_ve"], 1)
                    pool.wait_ge(s["ln_ve"], n + 1)
                    wait(pool, s["ln_out"], n)
                    nc.gpsimd.tensor_tensor(rstd[:], ve[:], halfpow[:, 1, 0:TILES], ALU.pow).then_inc(s["ln_rstd"], 1)
                if kind == "rscale":
                    pool.wait_ge(s["ms_done"], n + 1)
                    wait(pool, s["rden_done"], n)
                    nc.gpsimd.tensor_tensor(rms[:], ms[:], halfpow[:, 0, 0:TILES], ALU.pow).then_inc(s["rms_done"], 1)
                if kind == "root2":
                    pool.wait_ge(s["ln2_aggr"], n + 1)
                    settle(pool)
                    nc.gpsimd.tensor_scalar(pair[:, 0, :], moments2[:, :, 1], 0.0, None, ALU.add)
                    nc.gpsimd.tensor_scalar(pair[:, 1, :], moments2[:, :, 1], LN_EPS, None,
                                            ALU.add).then_inc(s["ln2_pair"], 1)
                    pool.wait_ge(s["ln2_pair"], n + 1)
                    nc.gpsimd.tensor_tensor(roots[:], pair[:], halfpow[:, 0:1, 0:TILES].to_broadcast([P, 2, TILES]),
                                            ALU.pow).then_inc(s["ln2_roots"], 1)

            run(pool, piece)

        @block.scalar
        def _(sc):
            def prepare(g):
                for n in chunks_of.get(g, ()):
                    _, hi_, _, cols = chunks[n]
                    sc.wait_ge(stage_in[n % 2], 16 * (n // 2 + 1))
                    nc.scalar.activation(hi_, stage_half[n % 2][:, 0:cols], ACT.Copy).then_inc(s["w_hi"], 1)
                if g == -3:
                    sc.wait_ge(s["merge_ps"], 1)
                    nc.scalar.activation(qk_h[:], SC[:, 0:DC * D].rearrange("p (a b) -> p a b", a=DC), ACT.Copy,
                                         scale=float(D) ** -0.5).then_inc(s["qk_ready"], 1)

            def hi(out, in_, done, got, freed, n):
                sc.wait_ge(got, n + 1)
                wait(sc, freed, n)
                nc.scalar.activation(out, in_, ACT.Copy).then_inc(done, 1)

            def square(n, k):
                j = FC * n + k
                sc.wait_ge(s["gelu_done"], j + 1)
                if k == 0:
                    wait(sc, s["ss_done"], n)
                    out = sqsum[:]
                else:
                    wait(sc, s["sqsum_done"], (FC - 1) * n + k - DEEP)
                    out = sq[:, k % DEEP, :]
                nc.scalar.activation(out, act[:, k % DEEP, :], ACT.Square).then_inc(s["sq_done"], 1)

            def piece(kind, k, n, sl, half):
                if kind == "gelu":
                    j = FC * n + k
                    sc.wait_ge(s["up_done"], j + 1)
                    wait_lo(sc, n, k - DEEP)
                    wait(sc, s["sq_done"], j + 1 - DEEP)
                    nc.scalar.activation(act[:, k % DEEP, :], ps[:, 6 + k % 2, 0:GT], ACT.Gelu).then_inc(s["gelu_done"], 1)
                    if k:
                        square(n, k - 1)
                    if k == FC - 1:
                        square(n, k)
                if kind == "exp_table":
                    wait(sc, s["warmed"], n)
                    nc.scalar.activation(warm[:], ones[:, 0:1], ACT.Exp).then_inc(s["warmed"], 1)
                if kind == "exp":
                    sc.wait_ge(s["negmax_done"], n + 1)
                    wait(sc, s["rinv_done"], n)
                    for i in range(TILES):
                        last = nc.scalar.activation(prob[:, i, :], prob[:, i, :], ACT.Exp, bias=negmax[:, i:i + 1],
                                                    accum_out=rowsum[:, i:i + 1])
                    last.then_inc(s["exp_done"], 1)
                if kind == "pT_split":
                    hi(pT_h[:], ps[:, 0:2, :].rearrange("p a b -> p (a b)")[:, 0:5 * P]
                       .rearrange("p (a b) -> p a b", a=5), s["pT_hi"], s["pT_done"], s["pv_done"], n)
                if kind == "x_split":
                    hi(xT_h[:], XT[:, :, 0:GT], s["x_hi"], s["xT_done"], s["v_done"], n)
                if kind == "t_split":
                    hi(tT_h[:], ps[:, 2:4, 0:GT], s["t_hi"], s["t_done"], s["score_done"], n)
                if kind == "v_split":
                    hi(v_h[:], VO[:, 0:TILES * D].rearrange("p (a b) -> p a b", a=TILES), s["v_hi"], s["v_done"],
                       s["pv_done"], n)
                if kind == "x2_split":
                    sc.wait_ge(s["x2T_done"], n + 1)
                    wait(sc, s["up_done"], FC * n)
                    nc.scalar.activation(x2_h[:], XT[:, :, 0:GT], ACT.Copy).then_inc(s["x2_hi"], 1)

            run(sc, piece, prepare)

        @block.vector
        def _(v):
            def ternary(n):
                out = tern[n][2]
                v.wait_ge(s["tern_in"], 16 * (n + 1))
                nc.vector.tensor_reduce(abparts[:], stage[:].rearrange("p (a b) -> p a b", a=32), AX_X, ALU.add,
                                        apply_absolute_value=True).then_inc(s["w_abs_parts"], 1)
                v.wait_ge(s["w_abs_parts"], n + 1)
                nc.vector.tensor_reduce(absum[:, n:n + 1], abparts[:], AX_X, ALU.add).then_inc(s["w_abs"], 1)
                v.wait_ge(s["w_alpha_ps"], n + 1)
                nc.vector.tensor_scalar(half_alpha[:, n:n + 1], ps[:, 7, n:n + 1], 0.5 / (D * FF), None,
                                        ALU.mult).then_inc(s["w_alpha"], 1)
                v.wait_ge(s["w_alpha"], n + 1)
                for part in range(2):
                    col = slice(1024 * part, 1024 * part + 1024)
                    k = 2 * n + part
                    wait(v, s["w_sum"], k)
                    nc.vector.tensor_scalar(tern_tmp, stage[:, col], -1.0, half_alpha[:, n:n + 1], ALU.mult,
                                            ALU.is_gt).then_inc(s["w_sign"], 1)
                    v.wait_ge(s["w_sign"], k + 1)
                    last = nc.vector.scalar_tensor_tensor(out=out[:, col], in0=stage[:, col],
                                                          scalar=half_alpha[:, n:n + 1], in1=tern_tmp,
                                                          op0=ALU.is_gt, op1=ALU.subtract)
                    last.then_inc(s["w_sum"], 1)

            def prepare(g):
                for n in chunks_of.get(g, ()):
                    _, hi_, lo_, cols = chunks[n]
                    v.wait_ge(s["w_hi"], n + 1)
                    nc.vector.tensor_tensor(lo_, stage_half[n % 2][:, 0:cols], hi_.bitcast(F32),
                                            ALU.subtract).then_inc(s["w_lo"], 1)
                if g == -3:
                    v.wait_ge(s["qk_ready"], 1)
                    nc.vector.scalar_tensor_tensor(out=qk_l[:], in0=SC[:, 0:DC * D].rearrange("p (a b) -> p a b", a=DC),
                                                   scalar=float(D) ** -0.5, in1=qk_h[:].bitcast(F32), op0=ALU.mult,
                                                   op1=ALU.subtract).then_inc(s["qk_ready"], 1)
                    v.wait_ge(s["const_in"], 16)
                    v.wait_ge(s["mask_ready"], 1)

            def lo(out, in_, hi_, got, done, n):
                v.wait_ge(got, n + 1)
                nc.vector.tensor_tensor(out, in_, hi_, ALU.subtract).then_inc(done, 1)

            def piece(kind, k, n, sl, half):
                if kind == "gelu":
                    j = FC * n + k
                    v.wait_ge(s["gelu_done"], j + 1)
                    if k == 0:
                        wait(v, s["down_done"], 2 * n)
                    nc.vector.tensor_copy(act_h[:, k, :], act[:, k % DEEP, :]).then_inc(s["ffn_hi"], 1)
                    if k in lo_vector:
                        v.wait_ge(s["ffn_hi"], j + 1)
                        nc.vector.tensor_tensor(act_l[:, k, :], act[:, k % DEEP, :], act_h[:, k, :].bitcast(F32),
                                                ALU.subtract).then_inc(s["ffn_lo_v"], 1)
                if kind == "add":
                    v.wait_ge(s["sq_done"], FC * n + k + 1)
                    if k > 1:
                        v.wait_ge(s["sqsum_done"], (FC - 1) * n + k - 1)
                    nc.vector.tensor_tensor(sqsum[:], sqsum[:], sq[:, k % DEEP, :], ALU.add).then_inc(s["sqsum_done"], 1)
                if kind == "x_split":
                    lo(xT_l[:], XT[:, :, 0:GT], xT_h[:].bitcast(F32), s["x_hi"], s["x_lo"], n)
                if kind == "t_split":
                    lo(tT_l[:], ps[:, 2:4, 0:GT], tT_h[:].bitcast(F32), s["t_hi"], s["t_lo"], n)
                if kind == "v_split":
                    lo(v_l[:], VO[:, 0:TILES * D].rearrange("p (a b) -> p a b", a=TILES), v_h[:].bitcast(F32),
                       s["v_hi"], s["v_lo"], n)
                if kind == "x2_split":
                    lo(x2_l[:], XT[:, :, 0:GT], x2_h[:].bitcast(F32), s["x2_hi"], s["x2_lo"], n)
                if kind == "pT_split":
                    lo(pT_l[:], ps[:, 0:2, :].rearrange("p a b -> p (a b)")[:, 0:5 * P]
                       .rearrange("p (a b) -> p a b", a=5), pT_h[:].bitcast(F32), s["pT_hi"], s["pT_lo"], n)
                    nc.vector.reciprocal(rinv[:], rowsum[:]).then_inc(s["rinv_done"], 1)
                if kind == "patch_split":
                    v.wait_ge(s["patch_in"], 16 * (n + 1))
                    wait(v, s["tok_done"], n)
                    nc.vector.tensor_copy(pat_h[:], patches[:]).then_inc(s["patch_hi"], 1)
                if kind == "ternary" and isinstance(n, int) and n == 0:
                    ternary(k)
                if kind == "max":
                    v.wait_ge(s["score_done"], n + 1)
                    wait(v, s["pT_done"], n)
                    settle(v)
                    for i in range(TILES):
                        last = nc.vector.tensor_tensor_reduce(prob[:, i, :], SC[:, i * D:(i + 1) * D], mask[:, i, :],
                                                              1.0, MASKED, ALU.add, ALU.max, rowmax[:, i:i + 1])
                    last.then_inc(s["max_done"], 1)
                    v.wait_ge(s["max_done"], n + 1)
                    nc.vector.tensor_scalar(negmax[:], rowmax[:], -1.0, None, ALU.mult).then_inc(s["negmax_done"], 1)
                if kind == "emb":
                    v.wait_ge(s["tok_done"], n + 1)
                    wait(v, s["h1_done"], n - 1)
                    nc.vector.tensor_tensor(emb[:, sl, 0, :], ps[:, 2, 0:D], bias_tok[:], ALU.add).then_inc(s["emb_img"], 1)
                    v.wait_ge(text_in[sl], 32 * (half + 1))
                    v.wait_ge(s["emb_img"], n + 1)
                    for i in range(TILES):
                        last = nc.vector.bn_stats(stats[:, i, :], emb[:, sl, i, :])
                    last.then_inc(s["ln_stats"], 1)
                    v.wait_ge(s["ln_stats"], n + 1)
                    settle(v)
                    for i in range(TILES):
                        last = nc.vector.bn_aggr(moments[:, i, :], stats[:, i, :])
                    last.then_inc(s["ln_aggr"], 1)
                if kind == "apply1":
                    v.wait_ge(s["ln_rstd"], n + 1)
                    v.wait_ge(s["ln_aggr"], n + 1)
                    wait(v, s["xT_done"], n)
                    for i in range(TILES):
                        last = nc.vector.tensor_scalar(xn[:, i, :], emb[:, sl, i, :], moments[:, i, 0:1],
                                                       rstd[:, i:i + 1], ALU.subtract, ALU.mult)
                    last.then_inc(s["ln_out"], 1)
                if kind == "ss":
                    v.wait_ge(s["ss_done"], n + 1)
                    nc.vector.tensor_scalar(ms[:], ps[:, 5, D:D + TILES], 1.0 / FF, None, ALU.mult).then_inc(s["ms_done"], 1)
                if kind == "h1":
                    v.wait_ge(s["pv_done"], n + 1)
                    v.wait_ge(s["rinv_done"], n + 1)
                    wait(v, s["stored"], 64 * (n - 1))
                    for i in range(TILES):
                        last = nc.vector.scalar_tensor_tensor(out=h[:, sl, i, :], in0=VO[:, i * D:(i + 1) * D],
                                                              scalar=rinv[:, i:i + 1], in1=emb[:, sl, i, :],
                                                              op0=ALU.mult, op1=ALU.add)
                    last.then_inc(s["h1_done"], 1)
                    v.wait_ge(s["h1_done"], n + 1)
                    for i in range(TILES):
                        last = nc.vector.bn_stats(stats2[:, i, :], h[:, sl, i, :])
                    last.then_inc(s["ln2_stats"], 1)
                    v.wait_ge(s["ln2_stats"], n + 1)
                    settle(v)
                    for i in range(TILES):
                        last = nc.vector.bn_aggr(moments2[:, i, :], stats2[:, i, :])
                    last.then_inc(s["ln2_aggr"], 1)
                if kind == "rscale":
                    v.wait_ge(s["rms_done"], n + 1)
                    nc.vector.tensor_scalar(rden[:], rms[:], RMS_EPS, None, ALU.add).then_inc(s["rden_done"], 1)
                    v.wait_ge(s["rden_done"], n + 1)
                    nc.vector.reciprocal(rscale[:], rden[:]).then_inc(s["rscale_done"], 1)
                if kind == "scale2":
                    v.wait_ge(s["ln2_roots"], n + 1)
                    nc.vector.scalar_tensor_tensor(out=den2[:], in0=roots[:, 1, :], scalar=RMS_EPS, in1=roots[:, 0, :],
                                                   op0=ALU.mult, op1=ALU.add).then_inc(s["ln2_den"], 1)
                    v.wait_ge(s["ln2_den"], n + 1)
                    nc.vector.reciprocal(scale2[:], den2[:]).then_inc(s["ln2_scale"], 1)
                    v.wait_ge(s["ln2_scale"], n + 1)
                    wait(v, s["x2T_done"], n)
                    for i in range(TILES):
                        last = nc.vector.tensor_scalar(xn2[:, i, :], h[:, sl, i, :], moments2[:, i, 0:1],
                                                       scale2[:, i:i + 1], ALU.subtract, ALU.mult)
                    last.then_inc(s["ln2_out"], 1)
                if kind == "h2":
                    if k != 1:
                        v.wait_ge(s["down_done"], 2 * n + 1 + k // 2)
                    v.wait_ge(s["rscale_done"], n + 1)
                    nc.vector.scalar_tensor_tensor(out=h[:, sl, k, :], in0=ps[:, 6 + k // 2, (k % 2) * D:(k % 2 + 1) * D],
                                                   scalar=rscale[:, k:k + 1], in1=h[:, sl, k, :], op0=ALU.mult,
                                                   op1=ALU.add).then_inc(s["h2_done"], 1)

            run(v, piece, prepare)

        @block.tensor
        def _(pe):
            def prepare(g):
                if g == -3:
                    pe.wait_ge(s["qk_in"], 32)
                    for m in range(DC):
                        for k in range(DC):
                            last = nc.tensor.matmul(SC[:, m * D:(m + 1) * D], wq[:, k, m * P:(m + 1) * P], wk[:, k, :],
                                                    start=(k == 0), stop=(k == DC - 1))
                    last.then_inc(s["merge_ps"], 1)

            def product(out, terms):
                for n, (a, b) in enumerate(terms):
                    last = nc.tensor.matmul(out, a, b, start=(n == 0), stop=(n == len(terms) - 1))
                return last

            def three(lh, ll, rh, rl, chunks_):
                return [t for k in chunks_ for t in ((lh(k), rh(k)), (lh(k), rl(k)), (ll(k), rh(k)))]

            def turn(x, done):
                for i in range(TILES):
                    for c in range(DC):
                        last = nc.tensor.transpose(XT[:, c, i * P:(i + 1) * P], x[:, i, c * P:(c + 1) * P], ident[:])
                last.then_inc(done, 1)

            def keys(x, k, i):
                if i < 2:
                    return x[:, k, 0:2 * P]
                return x[:, k, :].rearrange("p (t c) -> p t c", t=TILES)[:, 0:3:2, :]

            def piece(kind, k, n, sl, half):
                if kind == "ternary" and isinstance(n, int) and n == 0:
                    pe.wait_ge(s["w_abs"], k + 1)
                    nc.tensor.matmul(ps[:, 7, k:k + 1], ones[:], absum[:, k:k + 1], start=True,
                                     stop=True).then_inc(s["w_alpha_ps"], 1)
                if kind == "up":
                    if k < 2:
                        wait(pe, s["h2_done"], TILES * n - 1 + k)
                        pe.wait_ge(s["x2_lo"], n + 1)
                        if isinstance(n, int) and n == 0 and k == 0:
                            pe.wait_ge(s["w_sum"], 4)
                    else:
                        pe.wait_ge(s["gelu_done"], FC * n + k - 1)
                    w = up_w[:]
                    product(ps[:, 6 + k % 2, 0:GT],
                            [(w[:, kk, k * P:(k + 1) * P], x[:, kk, :]) for kk in range(DC) for x in (x2_h, x2_l)]
                            ).then_inc(s["up_done"], 1)
                if kind == "down":
                    if k < 2:
                        pe.wait_ge(s["gelu_done"], FC * n + 7)
                    else:
                        pe.wait_ge(s["gelu_done"], FC * n + FC)
                    for c in range(FC):
                        if k == 0:
                            wait_lo(pe, n, c)
                        for x in (act_h, act_l):
                            last = nc.tensor.matmul(ps[:, 6 + k // 2, (k % 2) * D:(k % 2 + 1) * D],
                                                    x[:, c, k * P:(k + 1) * P], dn_w[:, c, :],
                                                    start=(c == 0 and x is act_h), stop=(c == FC - 1 and x is act_l))
                    if k > 0:
                        last.then_inc(s["down_done"], 1)
                if kind == "ss":
                    pe.wait_ge(s["sqsum_done"], (FC - 1) * (n + 1))
                    pe.wait_ge(s["h1_done"], existing(n + 1))
                    for i in range(TILES):
                        last = nc.tensor.matmul(ps[:, 5, D + i:D + i + 1], sqsum[:, i * P:(i + 1) * P], ones[:, 0:1],
                                                start=True, stop=True)
                    last.then_inc(s["ss_done"], 1)
                if kind == "tok":
                    pe.wait_ge(s["patch_lo"], n + 1)
                    wait(pe, s["max_done"], n)
                    if isinstance(n, int) and n == 0:
                        pe.wait_ge(s["w_lo"], 2)
                    product(ps[:, 2, 0:D], three(lambda c: pat_h[:, c, :], lambda c: pat_l[:, c, :],
                                                 lambda c: tok_h[:, c, :], lambda c: tok_l[:, c, :],
                                                 range(KPC))).then_inc(s["tok_done"], 1)
                if kind == "xT":
                    pe.wait_ge(s["ln_out"], n + 1)
                    wait(pe, s["pT_lo"], n)
                    turn(xn, s["xT_done"])
                if kind == "t":
                    pe.wait_ge(s["x_lo"], n + 1)
                    pe.wait_ge(s["emb_img"], n + 1)
                    if isinstance(n, int) and n == 0:
                        pe.wait_ge(s["qk_ready"], 2)
                    for mm in range(DC):
                        last = product(ps[:, 2 + mm, 0:GT],
                                       three(lambda c: qk_h[:, c, mm * P:(mm + 1) * P],
                                             lambda c: qk_l[:, c, mm * P:(mm + 1) * P],
                                             lambda c: xT_h[:, c, :], lambda c: xT_l[:, c, :], range(DC)))
                    last.then_inc(s["t_done"], 1)
                if kind == "v":
                    pe.wait_ge(s["x_lo"], n + 1)
                    wait(pe, s["h1_done"], n)
                    wait(pe, s["ms_done"], n - 1)
                    if isinstance(n, int) and n == 0:
                        pe.wait_ge(s["w_lo"], 3)
                    for i in range(TILES):
                        last = product(VO[:, i * D:(i + 1) * D],
                                       three(lambda c: xT_h[:, c, i * P:(i + 1) * P],
                                             lambda c: xT_l[:, c, i * P:(i + 1) * P],
                                             lambda c: wv_h[:, c, :], lambda c: wv_l[:, c, :], range(DC)))
                    last.then_inc(s["v_done"], 1)
                if kind == "score":
                    pe.wait_ge(s["t_lo"], n + 1)
                    for i in range(TILES):
                        last = product(SC[:, i * D:(i + 1) * D],
                                       three(lambda c: tT_h[:, c, i * P:(i + 1) * P],
                                             lambda c: tT_l[:, c, i * P:(i + 1) * P],
                                             lambda c: keys(xT_h, c, i), lambda c: keys(xT_l, c, i), range(DC)))
                    last.then_inc(s["score_done"], 1)
                if kind == "pT":
                    pe.wait_ge(s["exp_done"], n + 1)
                    wait(pe, s["x2_lo"], n)
                    pairs = ((0, 0), (1, 0), (1, 1), (2, 0), (2, 1))
                    for j, (i, part) in enumerate(pairs):
                        last = nc.tensor.transpose(ps[:, j // 4, (j % 4) * P:(j % 4 + 1) * P],
                                                   prob[:, i, part * P:(part + 1) * P], ident[:])
                    last.then_inc(s["pT_done"], 1)
                if kind == "pv":
                    pe.wait_ge(s["pT_lo"], n + 1)
                    pe.wait_ge(s["v_lo"], n + 1)
                    terms = (((0, 0),), ((1, 0), (2, 1)), ((3, 0), (4, 2)))
                    for i in range(TILES):
                        last = product(VO[:, i * D:(i + 1) * D],
                                       [t for blk, kt in terms[i] for t in (
                                           (pT_h[:, blk, :], v_h[:, kt, :]), (pT_h[:, blk, :], v_l[:, kt, :]),
                                           (pT_l[:, blk, :], v_h[:, kt, :]))])
                    last.then_inc(s["pv_done"], 1)
                if kind == "x2T":
                    pe.wait_ge(s["ln2_out"], n + 1)
                    pe.wait_ge(s["x_lo"], existing(n + 1))
                    turn(xn2, s["x2T_done"])

            run(pe, piece, prepare)


def part_b(nc, W, io, consts):
    with ExitStack() as ctx:
        def sb(name, shape, dt=F32):
            return ctx.enter_context(nc.sbuf_tensor(name, shape, dt))

        ident, ones, halfpow = consts.ident, consts.ones, consts.halfpow
        ln_in = sb("B_ln_in", [P, BTILES, D])
        res = sb("B_residual", [P, 2, BTILES, D])
        stats, moments = sb("B_stats", [P, BTILES, 6]), sb("B_moments", [P, BTILES, 2])
        ve, rstd = sb("B_var_eps", [P, BTILES]), sb("B_rstd", [P, BTILES])
        x_h, x_l = sb("B_x_hi", [P, DC, BT], F32R), sb("B_x_lo", [P, DC, BT], F32R)
        xi_h, xi_l = sb("B_xi_hi", [P, IC, BT], F32R), sb("B_xi_lo", [P, IC, BT], F32R)
        drive = sb("B_xi_then_drive", [P, 2, IC, BT])
        lam = sb("B_lam", [P, 2, IC, BT])
        vv_ = sb("B_v", [P, 2, IC, BT])
        refl = sb("B_reflection", [P, 2, IC, BT])
        gate = sb("B_gate", [P, 2, IC, BT])
        tmp = sb("B_tanh", [P, 2, BT])
        vsq = sb("B_v_squared", [P, BT])
        vsum = sb("B_v_squared_sum", [P, BT])
        inv = sb("B_two_over_vv", [P, BT])
        hs = sb("B_states", [P, IC, BT])
        prod, m_, g_, w_ = (sb("B_" + x, [P, IC, NB]) for x in ("prod", "decayed", "driven", "reflected"))
        dots = sb("B_dots", [P, NB])
        ytmp = sb("B_y", [P, IC, P])
        y_h, y_l = sb("B_y_hi", [P, 2, IC, P], F32R), sb("B_y_lo", [P, 2, IC, P], F32R)
        vec = sb("B_channel_vectors", [P, 3, IC])
        sp_ = sb("B_softplus", [P, 8, IC])
        ps = ctx.enter_context(nc.psum_tensor("psB", [P, 8, 512], F32))

        s = {}
        for name in """ln_in res_in0 res_in1 ln_stats ln_aggr ln_ve ln_rstd ln_out xT_done x_hi x_lo win_done l_done vproj_done
                xi_copy xi_hi xi_lo z_tanh z_gate l_tanh lam_done lam_first drive_done v_done vsq_done vsum_done vv_done inv_done
                lv_done refl_done prod_done decay_done driven_done dot_done sum_done w_done h_done y_done y_hi y_lo
                wout_done res_done stored vec_in half_ready c1 c2 c3 c4 c5 c6 c7 h_zero""".split():
            s[name] = ctx.enter_context(nc.semaphore("B_" + name))

        res_in = [s["res_in0"], s["res_in1"]]

        def at(q, r):
            return slice(q * P + r, (q + 1) * P, 4)

        def tile(q):
            return slice(q * P, (q + 1) * P)

        order = """load_ln.0 xi.0 xi.1 vv.0 inv.0 start.0 xi.2 inv.1 inv.2 inv.3 xi.3 late_wout.3 scan.0 late_res.3 load_res.0
                z.0 z.1 z.2 scan.1  z.3 z.4 z.5 gate.0 scan.2  z.6 z.7 gate.1 l.0 scan.3 y.0  l.1 l.2 l.3 gate.2 scan.4
                ysplit.0 l.4 l.5 l.6 gate.3 scan.5  l.7 l.8 l.9 drive.0 scan.6  l.10 wout.0 stats.0 scan.7 y.1
                l.11 l.12 l.13 res.0 drive.1 scan.8  ysplit.1 l.14 l.15 v.0 stats.1 ln.0 scan.9  v.1 v.2 v.3 drive.2 scan.10
                wout.1 v.4 drive.3 scan.11 y.2  v.5 v.6 v.7 res.1 apply.0 scan.12  ysplit.2 apply.1 v.8 v.9 v.10 scan.13
                turn.0 v.11 v.12 vsum.1 scan.14  wout.2 v.13 res.2 turned.0 scan.15 turned.1 y.3  v.14 v.15 vsum.2
                ysplit.3 vsum.3""".split()
        order = [(kind, int(k)) for kind, k in (w.split(".") for w in order)]

        def part_of(kind):
            return {"xi": 1, "z": 1, "gate": 1, "l": 1, "v": 1, "drive": 1, "vsum": 1, "load_res": 1, "late_wout": -1, "late_res": -1,
                    "stats": 2, "ln": 2, "apply": 2, "turn": 2, "turned": 2, "load_ln": 2}.get(kind, 0)

        def run(eng, piece):
            def step(n, sl, half):
                for kind, k in order:
                    off = part_of(kind)
                    if not isinstance(n, int) or 0 <= n + off < BLOCKS:
                        piece(kind.removeprefix("late_"), k, n + off, (sl + off) % 2, half + (sl + off) // 2)

            for n in (-2, -1, 0, 1):
                step(n, n % 2, n // 2)
            with eng.Fori(1, BLOCKS // 2 - 1) as half_:
                step(2 * half_, 0, half_)
                step(2 * half_ + 1, 1, half_)
            for n in (BLOCKS - 2, BLOCKS - 1, BLOCKS):
                step(n, n % 2, n // 2)

        def bank(j):
            return (2, 3, 4, 2, 3, 4, 2, 5, 3, 4, 2, 3, 4, 2, 3, 5)[j]

        block = ctx.enter_context(nc.Block())

        def rows(t, n, q=None):
            if q is None:
                return t[:, bass.ds(n * STEPS, STEPS), :].rearrange("b (q r) d -> q b r d", q=BTILES)
            return t[:, bass.ds(n * STEPS + 4 * q, 4), :]

        @block.sync
        def _(sp):
            sp.dma_start(vec[:], io["vectors"]).then_inc(s["vec_in"], 16)

            def piece(kind, k, n, sl, half):
                if kind == "load_ln":
                    wait(sp, s["xT_done"], n)
                    for q in range(BTILES):
                        sp.dma_start(ln_in[:, q, :], rows(io["h2"], n, q)).then_inc(s["ln_in"], 16)
                if kind == "load_res":
                    wait(sp, s["stored"], 64 * (n - 1))
                    for q in range(BTILES):
                        sp.dma_start(res[:, sl, q, :], rows(io["h2"], n, q)).then_inc(res_in[sl], 16)
                if kind == "res":
                    sp.wait_ge(s["res_done"], 4 * n + k + 1)
                    sp.dma_start(rows(io["out"], n, k), res[:, sl, k, :]).then_inc(s["stored"], 16)

            run(sp, piece)
            sp.wait_ge(s["stored"], 64 * BLOCKS)

        @block.gpsimd
        def _(pool):
            def piece(kind, k, n, sl, half):
                if kind == "xi":
                    pool.wait_ge(s["xi_hi"], 4 * n + k + 1)
                    nc.gpsimd.tensor_tensor(xi_l[:, k, :], drive[:, sl, k, :], xi_h[:, k, :].bitcast(F32),
                                            ALU.subtract).then_inc(s["xi_lo"], 1)
                if kind == "v" and k % IC == IC - 1:
                    m = k // IC
                    pool.wait_ge(s["v_done"], 4 * n + m + 1)
                    pool.wait_ge(s["lam_done"], 4 * n + m + 1)
                    if isinstance(n, int) and n == 0:
                        pool.wait_ge(s["lam_first"], m + 1)
                    wait(pool, s["h_done"], 16 * (n - 1))
                    nc.gpsimd.tensor_tensor(refl[:, sl, m, :], lam[:, sl, m, :], vv_[:, sl, m, :],
                                            ALU.mult).then_inc(s["lv_done"], 1)
                if kind == "inv":
                    pool.wait_ge(s["inv_done"], 4 * n + k + 1)
                    pool.wait_ge(s["lv_done"], 4 * n + 4)
                    part = refl[:, sl, :, tile(k)]
                    nc.gpsimd.tensor_tensor(part, part, inv[:, tile(k)].rearrange("p (o b) -> p o b", o=1)
                                            .to_broadcast([P, IC, P]), ALU.mult).then_inc(s["refl_done"], 1)
                if kind == "y":
                    pool.wait_ge(s["h_done"], 16 * n + 4 * k + 4)
                    pool.wait_ge(s["z_gate"], 4 * n + 4)
                    wait(pool, s["y_lo"], 4 * n + k)
                    nc.gpsimd.tensor_tensor(ytmp[:], gate[:, sl, :, tile(k)], hs[:, :, tile(k)],
                                            ALU.mult).then_inc(s["y_done"], 1)
                if kind == "ysplit":
                    pool.wait_ge(s["y_hi"], 4 * n + k + 1)
                    nc.gpsimd.tensor_tensor(y_l[:, k % 2, :, :], ytmp[:], y_h[:, k % 2, :, :].bitcast(F32),
                                            ALU.subtract).then_inc(s["y_lo"], 1)
                if kind == "ln":
                    pool.wait_ge(s["ln_aggr"], n + 1)
                    settle(pool)
                    nc.gpsimd.tensor_scalar(ve[:], moments[:, :, 1], LN_EPS, None, ALU.add).then_inc(s["ln_ve"], 1)
                    pool.wait_ge(s["ln_ve"], n + 1)
                    wait(pool, s["ln_out"], 2 * n)
                    nc.gpsimd.tensor_tensor(rstd[:], ve[:], halfpow[:, 1, 0:BTILES], ALU.pow).then_inc(s["ln_rstd"], 1)

            run(pool, piece)

        @block.scalar
        def _(sc):
            sc.wait_ge(s["c1"], 1)
            nc.scalar.activation(sp_[:, 1, :], sp_[:, 0, :], ACT.Exp, scale=-1.0).then_inc(s["c2"], 1)
            sc.wait_ge(s["c3"], 1)
            nc.scalar.activation(sp_[:, 3, :], sp_[:, 2, :], ACT.Ln).then_inc(s["c4"], 1)
            sc.wait_ge(s["half_ready"], 2)

            def piece(kind, k, n, sl, half):
                if kind == "xi":
                    sc.wait_ge(s["win_done"], 8 * n + k + 1)
                    wait(sc, s["h_done"], 16 * (n - 1))
                    nc.scalar.activation(drive[:, sl, k, :], ps[:, bank(k), :], ACT.Copy).then_inc(s["xi_copy"], 1)
                    wait(sc, s["vproj_done"], 4 * n)
                    nc.scalar.activation(xi_h[:, k, :], ps[:, bank(k), :], ACT.Copy).then_inc(s["xi_hi"], 1)
                if kind == "z" and k % DC == DC - 1:
                    m = k // DC
                    sc.wait_ge(s["win_done"], 8 * n + 4 + m + 1)
                    wait(sc, s["z_gate"], 4 * n + m - 1)
                    if m < 2:
                        wait(sc, s["lam_done"], 4 * n)
                    nc.scalar.activation(tmp[:, m % 2, :], ps[:, bank(4 + m), :], ACT.Tanh,
                                         scale=0.5).then_inc(s["z_tanh"], 1)
                if kind == "l" and k % IC == IC - 1:
                    m = k // IC
                    sc.wait_ge(s["l_done"], 4 * n + m + 1)
                    if m < 2:
                        sc.wait_ge(s["z_gate"], 4 * n + 3 + m)
                    else:
                        sc.wait_ge(s["lam_done"], 4 * n + m - 1)
                    nc.scalar.activation(tmp[:, m % 2, :], ps[:, bank(8 + m), :], ACT.Tanh, scale=0.5,
                                         bias=vec[:, 1, m:m + 1]).then_inc(s["l_tanh"], 1)
                    sc.wait_ge(s["l_tanh"], 4 * n + m + 1)
                    wait(sc, s["h_done"], 16 * (n - 1))
                    nc.scalar.activation(lam[:, sl, m, :], tmp[:, m % 2, :], ACT.Exp, scale=sp_[:, 7, m:m + 1],
                                         bias=sp_[:, 7, m:m + 1]).then_inc(s["lam_done"], 1)
                if kind == "v" and k % IC == IC - 1:
                    m = k // IC
                    sc.wait_ge(s["vproj_done"], 4 * n + m + 1)
                    if m == 0:
                        wait(sc, s["vv_done"], n)
                        out = vsum
                    else:
                        wait(sc, s["vsum_done"], 3 * n + m - 1)
                        out = vsq
                    nc.scalar.activation(out[:], ps[:, bank(12 + m), :], ACT.Square,
                                         bias=vec[:, 2, m:m + 1]).then_inc(s["vsq_done"], 1)
                    nc.scalar.activation(vv_[:, sl, m, :], ps[:, bank(12 + m), :], ACT.Identity,
                                         bias=vec[:, 2, m:m + 1]).then_inc(s["v_done"], 1)
                if kind == "ysplit":
                    sc.wait_ge(s["y_done"], 4 * n + k + 1)
                    wait(sc, s["wout_done"], 4 * n + k - 1)
                    nc.scalar.activation(y_h[:, k % 2, :, :], ytmp[:], ACT.Copy).then_inc(s["y_hi"], 1)
                if kind == "turned":
                    sc.wait_ge(s["xT_done"], n + 1)
                    wait(sc, s["win_done"], 8 * n)
                    nc.scalar.activation(x_h[:, k, :], ps[:, k, :], ACT.Copy).then_inc(s["x_hi"], 1)

            run(sc, piece)

        @block.vector
        def _(v):
            v.wait_ge(s["vec_in"], 16)
            omega = vec[:, 0, :]
            nc.vector.scalar_tensor_tensor(out=sp_[:, 0, :], in0=omega, scalar=-1.0, in1=omega, op0=ALU.mult,
                                           op1=ALU.max).then_inc(s["c1"], 1)
            nc.vector.tensor_scalar(vec[:, 1, :], vec[:, 1, :], 0.5, None, ALU.mult).then_inc(s["half_ready"], 1)
            nc.vector.memset(hs[:], 0.0).then_inc(s["h_zero"], 1)
            v.wait_ge(s["c2"], 1)
            nc.vector.tensor_scalar(sp_[:, 2, :], sp_[:, 1, :], 1.0, None, ALU.add).then_inc(s["c3"], 1)
            v.wait_ge(s["c3"], 1)
            v.wait_ge(s["c4"], 1)
            nc.vector.tensor_scalar(sp_[:, 4, :], sp_[:, 2, :], -1.0, None, ALU.add).then_inc(s["c5"], 1)
            v.wait_ge(s["c5"], 1)
            nc.vector.tensor_scalar(sp_[:, 5, :], sp_[:, 4, :], 0.0, None, ALU.is_equal).then_inc(s["c5"], 1)
            v.wait_ge(s["c5"], 2)
            nc.vector.tensor_tensor(sp_[:, 4, :], sp_[:, 4, :], sp_[:, 5, :], ALU.add).then_inc(s["c5"], 1)
            nc.vector.tensor_tensor(sp_[:, 3, :], sp_[:, 3, :], sp_[:, 5, :], ALU.add).then_inc(s["c5"], 1)
            v.wait_ge(s["c5"], 4)
            nc.vector.reciprocal(sp_[:, 6, :], sp_[:, 4, :]).then_inc(s["c6"], 1)
            nc.vector.tensor_tensor(sp_[:, 2, :], sp_[:, 1, :], sp_[:, 3, :], ALU.mult).then_inc(s["c6"], 1)
            v.wait_ge(s["c6"], 2)
            nc.vector.tensor_tensor(sp_[:, 0, :], sp_[:, 2, :], sp_[:, 6, :], ALU.mult).then_inc(s["c7"], 1)
            v.wait_ge(s["c7"], 1)
            nc.vector.scalar_tensor_tensor(out=sp_[:, 1, :], in0=omega, scalar=0.0, in1=sp_[:, 0, :], op0=ALU.max,
                                           op1=ALU.add).then_inc(s["c7"], 1)
            v.wait_ge(s["c7"], 2)
            nc.vector.tensor_scalar(sp_[:, 7, :], sp_[:, 1, :], -C_DECAY / 2, None, ALU.mult).then_inc(s["half_ready"], 1)
            v.wait_ge(s["h_zero"], 1)

            def col(buf, t):
                return buf[:, :, at(t // 4, t % 4)]

            def ahead(n, sl, t):
                prev = col(hs, (t - 1) % STEPS)
                wait(v, s["h_done"], 16 * n + t)
                nc.vector.tensor_tensor(prod[:], col(vv_[:, sl], t), prev, ALU.mult).then_inc(s["prod_done"], 1)
                nc.vector.tensor_tensor(m_[:], col(lam[:, sl], t), prev, ALU.mult).then_inc(s["decay_done"], 1)

            def piece(kind, k, n, sl, half):
                if kind == "gate":
                    v.wait_ge(s["z_tanh"], 4 * n + k + 1)
                    wait(v, s["y_done"], 4 * (n - 1))
                    nc.vector.scalar_tensor_tensor(out=gate[:, sl, k, :], in0=tmp[:, k % 2, :], scalar=1.0,
                                                   in1=ps[:, bank(4 + k), :], op0=ALU.add,
                                                   op1=ALU.mult).then_inc(s["z_gate"], 1)
                if kind == "drive":
                    v.wait_ge(s["lam_done"], 4 * n + k + 1)
                    if isinstance(n, int) and n == 0:
                        nc.vector.memset(lam[:, sl, k, at(0, 0)], 0.0).then_inc(s["lam_first"], 1)
                        v.wait_ge(s["lam_first"], k + 1)
                    v.wait_ge(s["xi_lo"], 4 * n + k + 1)
                    last = nc.vector.scalar_tensor_tensor(out=drive[:, sl, k, :], in0=lam[:, sl, k, :], scalar=1.0,
                                                          in1=drive[:, sl, k, :], op0=ALU.subtract, op1=ALU.mult)
                    last.then_inc(s["drive_done"], 1)
                if kind == "vsum":
                    v.wait_ge(s["vsq_done"], 4 * n + k + 1)
                    wait(v, s["vsum_done"], 3 * n + k - 1)
                    nc.vector.tensor_tensor(vsum[:], vsum[:], vsq[:], ALU.add).then_inc(s["vsum_done"], 1)
                if kind == "inv":
                    v.wait_ge(s["vv_done"], n + 1)
                    wait(v, s["refl_done"], 4 * (n - 1) + k + 1)
                    nc.vector.reciprocal(inv[:, tile(k)], ps[:, 5, tile(k)]).then_inc(s["inv_done"], 1)
                if kind == "start":
                    v.wait_ge(s["v_done"], 4 * n + 4)
                    v.wait_ge(s["drive_done"], 4 * n + 4)
                    ahead(n, sl, 0)
                if kind == "scan":
                    v.wait_ge(s["dot_done"], 16 * n + k + 1)
                    nc.vector.tensor_reduce(dots[:], ps[:, 7, 0:IC * NB].rearrange("p (g b) -> p b g", g=IC), AX_X,
                                            ALU.add).then_inc(s["sum_done"], 1)
                    v.wait_ge(s["decay_done"], 16 * n + k + 1)
                    nc.vector.tensor_tensor(g_[:], m_[:], col(drive[:, sl], k), ALU.subtract).then_inc(s["driven_done"], 1)
                    v.wait_ge(s["sum_done"], 16 * n + k + 1)
                    if k % 4 == 0:
                        v.wait_ge(s["refl_done"], 4 * n + k // 4 + 1)
                        wait(v, s["y_done"], 4 * (n - 1) + k // 4 + 1)
                    nc.vector.tensor_tensor(w_[:], col(refl[:, sl], k),
                                            dots[:].rearrange("p (o b) -> p o b", o=1).to_broadcast([P, IC, NB]),
                                            ALU.mult).then_inc(s["w_done"], 1)
                    v.wait_ge(s["w_done"], 16 * n + k + 1)
                    v.wait_ge(s["driven_done"], 16 * n + k + 1)
                    nc.vector.tensor_tensor(col(hs, k), g_[:], w_[:], ALU.subtract).then_inc(s["h_done"], 1)
                    if k + 1 < STEPS:
                        ahead(n, sl, k + 1)
                if kind == "res":
                    v.wait_ge(s["wout_done"], 4 * n + k + 1)
                    v.wait_ge(res_in[sl], 64 * (half + 1))
                    nc.vector.scalar_tensor_tensor(out=res[:, sl, k, :], in0=ps[:, 6, (k % 2) * D:(k % 2 + 1) * D],
                                                   scalar=0.5, in1=res[:, sl, k, :], op0=ALU.mult,
                                                   op1=ALU.add).then_inc(s["res_done"], 1)
                if kind == "stats":
                    v.wait_ge(s["ln_in"], 64 * (n + 1))
                    for q in (2 * k, 2 * k + 1):
                        last = nc.vector.bn_stats(stats[:, q, :], ln_in[:, q, :])
                    last.then_inc(s["ln_stats"], 1)
                if kind == "ln":
                    v.wait_ge(s["ln_stats"], 2 * n + 2)
                    settle(v)
                    for q in range(BTILES):
                        last = nc.vector.bn_aggr(moments[:, q, :], stats[:, q, :])
                    last.then_inc(s["ln_aggr"], 1)
                if kind == "apply":
                    v.wait_ge(s["ln_rstd"], n + 1)
                    v.wait_ge(s["ln_aggr"], n + 1)
                    for q in (2 * k, 2 * k + 1):
                        last = nc.vector.tensor_scalar(ln_in[:, q, :], ln_in[:, q, :], moments[:, q, 0:1],
                                                       rstd[:, q:q + 1], ALU.subtract, ALU.mult)
                    last.then_inc(s["ln_out"], 1)
                if kind == "turned":
                    v.wait_ge(s["x_hi"], 2 * n + k + 1)
                    nc.vector.tensor_tensor(x_l[:, k, :], ps[:, k, :], x_h[:, k, :].bitcast(F32),
                                            ALU.subtract).then_inc(s["x_lo"], 1)

            run(v, piece)

        @block.tensor
        def _(pe):
            def part(out, lh, ll, rh, rl, ks, first_, last_):
                terms = [t for k in ks for t in ((lh(k), rh(k)), (lh(k), rl(k)), (ll(k), rh(k)))]
                for i, (a, b) in enumerate(terms):
                    last = nc.tensor.matmul(out, a, b, start=(first_ and i == 0), stop=(last_ and i == len(terms) - 1))
                return last

            def win(j, bank_, cs):
                return part(ps[:, bank_, :], lambda c: W.in_h[:, c, j * P:(j + 1) * P],
                            lambda c: W.in_l[:, c, j * P:(j + 1) * P],
                            lambda c: x_h[:, c, :], lambda c: x_l[:, c, :], cs, cs[0] == 0, cs[-1] == DC - 1)

            def project(wh, wl, m, bank_, c):
                return part(ps[:, bank_, :], lambda c: wh[:, c, m * P:(m + 1) * P], lambda c: wl[:, c, m * P:(m + 1) * P],
                            lambda c: xi_h[:, c, :], lambda c: xi_l[:, c, :], [c], c == 0, c == IC - 1)

            def piece(kind, k, n, sl, half):
                if kind == "xi":
                    pe.wait_ge(s["x_lo"], 2 * n + 2)
                    if k < 3:
                        wait(pe, s["v_done"], 4 * (n - 1) + (2, 3, 1)[k])
                    else:
                        pe.wait_ge(s["xi_hi"], 4 * n + 1)
                    win(k, bank(k), [0, 1]).then_inc(s["win_done"], 1)
                if kind == "z":
                    m, c = k // DC, k % DC
                    if c == 0 and m < 3:
                        pe.wait_ge(s["xi_hi"], 4 * n + m + 2)
                    elif c == 0:
                        wait(pe, s["inv_done"], 4 * n)
                    last = win(4 + m, bank(4 + m), [c])
                    if c == DC - 1:
                        last.then_inc(s["win_done"], 1)
                if kind == "l":
                    m, c = k // IC, k % IC
                    if m == 0:
                        pe.wait_ge(s["xi_lo"], 4 * n + c + 1)
                    if c == 0 and m < 3:
                        pe.wait_ge(s["z_gate"], 4 * n + m + 1)
                    elif c == 0:
                        pe.wait_ge(s["l_tanh"], 4 * n + 1)
                    last = project(W.l_h, W.l_l, m, bank(8 + m), c)
                    if c == IC - 1:
                        last.then_inc(s["l_done"], 1)
                if kind == "v":
                    m, c = k // IC, k % IC
                    if c == 0 and m < 3:
                        pe.wait_ge(s["l_tanh"], 4 * n + m + 2)
                    elif c == 0:
                        pe.wait_ge(s["z_gate"], 4 * n + 4)
                    last = project(W.v_h, W.v_l, m, bank(12 + m), c)
                    if c == IC - 1:
                        last.then_inc(s["vproj_done"], 1)
                if kind == "scan":
                    pe.wait_ge(s["prod_done"], 16 * n + k + 1)
                    wait(pe, s["sum_done"], 16 * n + k)
                    nc.tensor.matmul(ps[:, 7, 0:IC * NB], ones[:], prod[:].rearrange("p g b -> p (g b)"), start=True,
                                     stop=True).then_inc(s["dot_done"], 1)
                if kind == "vv":
                    pe.wait_ge(s["vsum_done"], 3 * n + 3)
                    pe.wait_ge(s["v_done"], 4 * n + 4)
                    nc.tensor.matmul(ps[:, 5, :], consts.halves[:], vsum[:], start=True, stop=True).then_inc(s["vv_done"], 1)
                if kind == "wout":
                    pe.wait_ge(s["y_lo"], 4 * n + k + 1)
                    wait(pe, s["res_done"], 4 * n + k)
                    part(ps[:, 6, (k % 2) * D:(k % 2 + 1) * D], lambda c: y_h[:, k % 2, c, :],
                         lambda c: y_l[:, k % 2, c, :], lambda c: W.out_h[:, c, :], lambda c: W.out_l[:, c, :],
                         range(IC), True, True).then_inc(s["wout_done"], 1)
                if kind == "turn":
                    pe.wait_ge(s["ln_out"], 2 * n + 2)
                    wait(pe, s["x_lo"], 2 * n)
                    for q in range(BTILES):
                        for c in range(DC):
                            last = nc.tensor.transpose(ps[:, c, tile(q)], ln_in[:, q, c * P:(c + 1) * P], ident[:])
                    last.then_inc(s["xT_done"], 1)

            run(pe, piece)


def part_c(nc, io, consts):
    MQ = MT // P
    SLOTS = 4
    with ExitStack() as ctx:
        def sb(name, shape, dt=F32):
            return ctx.enter_context(nc.sbuf_tensor(name, shape, dt))

        ident, halfpow = consts.ident, consts.halfpow
        acc, xn = sb("C_residual", [P, MQ, D]), sb("C_normed", [P, MQ, D])
        stats, moments = sb("C_stats", [P, MQ, 6]), sb("C_moments", [P, MQ, 2])
        ve, rstd = sb("C_var_eps", [P, MQ]), sb("C_rstd", [P, MQ])
        x_h, x_l = sb("C_x_hi", [P, DC, MT], F32R), sb("C_x_lo", [P, DC, MT], F32R)
        picked, picked_f = sb("C_picked", [P, MQ, 2], I32), sb("C_picked_f", [P, MQ, 2])
        weights = sb("C_routing", [P, MQ, E_N])
        eq = sb("C_is_picked", [P, 2, MQ, E_N])
        wc = sb("C_weight", [P, MQ, E_N])
        wcT = sb("C_weightT", [E_N, MQ, P])
        b_up, b_dn = sb("C_up_bias", [P, E_N, 4]), sb("C_down_bias", [E_N, D])
        raw = sb("C_raw", [P, 2, 6 * D])
        w_h, w_l = sb("C_w_hi", [P, SLOTS, 6 * D], F32R), sb("C_w_lo", [P, SLOTS, 6 * D], F32R)
        gate, up, th, glu = (sb("C_" + x, [P, 2, MT]) for x in ("gate", "up", "tanh", "glu"))
        a_h, a_l = sb("C_act_hi", [P, 2, 2, MT], F32R), sb("C_act_lo", [P, 2, 2, MT], F32R)
        ps = ctx.enter_context(nc.psum_tensor("psC", [P, 8, 512], F32))
        s = {}
        for name in """h_in const_in raw_in0 raw_in1 stats aggr ve rstd normed xT x_hi x_lo cast eq eq_sum wc wcT wcT_copy
                bias bias_added w_hi w_lo gu gate_b up_b up_c tanh glu act a_hi a_lo down acc stored""".split():
            s[name] = ctx.enter_context(nc.semaphore("C_" + name))
        with nc.Block() as clearing:
            @clearing.sync
            def _(sp):
                for sem_ in s.values():
                    sp.sem_clear(sem_)
        raw_in = [s["raw_in0"], s["raw_in1"]]
        next_split = {0: 3, **{e: e + 2 for e in range(2, E_N - 2)}}
        rows = io["out"].rearrange("b t d -> (b t) d")[0:MT, :].rearrange("(q p) d -> p q d", p=P)
        block = ctx.enter_context(nc.Block())

        @block.sync
        def _(sp):
            sp.dma_start(acc[:], rows).then_inc(s["h_in"], 16)
            for a, b in ((picked, io["picked"]), (weights, io["routing"]), (b_up, io["up_bias"]), (b_dn, io["down_bias"])):
                sp.dma_start(a[:], b).then_inc(s["const_in"], 16)
            for e in range(E_N):
                if e >= 2:
                    sp.wait_ge(s["w_lo"], e - 1)
                sp.dma_start(raw[:, e % 2, :], io["experts"][e]).then_inc(raw_in[e % 2], 16)
            sp.wait_ge(s["acc"], MQ * E_N)
            sp.dma_start(rows, acc[:]).then_inc(s["stored"], 16)
            sp.wait_ge(s["stored"], 16)

        @block.gpsimd
        def _(pool):
            def split(e):
                pool.wait_ge(s["w_hi"], e + 1)
                nc.gpsimd.tensor_tensor(w_l[:, e % SLOTS, :], raw[:, e % 2, :], w_h[:, e % SLOTS, :].bitcast(F32),
                                        ALU.subtract).then_inc(s["w_lo"], 1)

            pool.wait_ge(s["aggr"], 1)
            nc.gpsimd.tensor_scalar(ve[:], moments[:, :, 1], LN_EPS, None, ALU.add).then_inc(s["ve"], 1)
            pool.wait_ge(s["ve"], 1)
            nc.gpsimd.tensor_tensor(rstd[:], ve[:], halfpow[:, 1, 0:MQ], ALU.pow).then_inc(s["rstd"], 1)
            for e in range(3):
                split(e)
            for e in range(E_N):
                pool.wait_ge(s["a_hi"], e + 1)
                nc.gpsimd.tensor_tensor(a_l[:, e % 2, :, :], glu[:], a_h[:, e % 2, :, :].bitcast(F32),
                                        ALU.subtract).then_inc(s["a_lo"], 1)
                if e in next_split:
                    split(next_split[e])

        @block.scalar
        def _(sc):
            def split(e):
                sc.wait_ge(raw_in[e % 2], 16 * (e // 2 + 1))
                if e >= SLOTS:
                    sc.wait_ge(s["down"], MQ * (e - SLOTS + 1))
                nc.scalar.activation(w_h[:, e % SLOTS, :], raw[:, e % 2, :], ACT.Copy).then_inc(s["w_hi"], 1)

            split(0)
            split(1)
            sc.wait_ge(s["xT"], 1)
            nc.scalar.activation(x_h[:], ps[:, 0:2, :], ACT.Copy).then_inc(s["x_hi"], 1)
            split(2)
            for e in range(E_N):
                for m in range(2):
                    sc.wait_ge(s["gate_b"], 2 * e + m + 1)
                    if e:
                        sc.wait_ge(s["glu"], 2 * (e - 1) + m + 1)
                    nc.scalar.activation(th[:, m, :], gate[:, m, :], ACT.Tanh, scale=ALPHA / 2).then_inc(s["tanh"], 1)
                sc.wait_ge(s["act"], 2 * e + 2)
                if e >= 2:
                    sc.wait_ge(s["down"], MQ * (e - 1))
                nc.scalar.activation(a_h[:, e % 2, :, :], glu[:], ACT.Copy).then_inc(s["a_hi"], 1)
                if e in next_split:
                    split(next_split[e])

        @block.vector
        def _(v):
            v.wait_ge(s["h_in"], 16)
            for q in range(MQ):
                last = nc.vector.bn_stats(stats[:, q, :], acc[:, q, :])
            last.then_inc(s["stats"], 1)
            v.wait_ge(s["stats"], 1)
            for q in range(MQ):
                last = nc.vector.bn_aggr(moments[:, q, :], stats[:, q, :])
            last.then_inc(s["aggr"], 1)
            v.wait_ge(s["const_in"], 64)
            nc.vector.tensor_copy(picked_f[:], picked[:]).then_inc(s["cast"], 1)
            v.wait_ge(s["cast"], 1)
            for k in range(2):
                for e in range(E_N):
                    last = nc.vector.tensor_scalar(eq[:, k, :, e], picked_f[:, :, k], float(e), None, ALU.is_equal)
            last.then_inc(s["eq"], 1)
            v.wait_ge(s["eq"], 1)
            nc.vector.tensor_tensor(wc[:], eq[:, 0], eq[:, 1], ALU.add).then_inc(s["eq_sum"], 1)
            v.wait_ge(s["eq_sum"], 1)
            nc.vector.tensor_tensor(wc[:], wc[:], weights[:], ALU.mult).then_inc(s["wc"], 1)
            v.wait_ge(s["rstd"], 1)
            v.wait_ge(s["aggr"], 1)
            for q in range(MQ):
                last = nc.vector.tensor_scalar(xn[:, q, :], acc[:, q, :], moments[:, q, 0:1], rstd[:, q:q + 1],
                                               ALU.subtract, ALU.mult)
            last.then_inc(s["normed"], 1)
            v.wait_ge(s["x_hi"], 1)
            nc.vector.tensor_tensor(x_l[:], ps[:, 0:2, :], x_h[:].bitcast(F32), ALU.subtract).then_inc(s["x_lo"], 1)
            v.wait_ge(s["wcT"], 1)
            nc.vector.tensor_copy(wcT[:].rearrange("p a b -> p (a b)"), ps[0:E_N, 6, :]).then_inc(s["wcT_copy"], 1)

            def combine(e):
                for q in range(MQ):
                    v.wait_ge(s["down"], MQ * e + q + 1)
                    wait(v, s["acc"], MQ * (e - 1) + q + 1)
                    nc.vector.scalar_tensor_tensor(out=acc[:, q, :], in0=ps[:, (6, 7, 0, 1)[q], 0:D],
                                                   scalar=wc[:, q, e:e + 1], in1=acc[:, q, :], op0=ALU.mult,
                                                   op1=ALU.add).then_inc(s["acc"], 1)

            for e in range(E_N):
                for m in range(2):
                    v.wait_ge(s["gu"], 4 * e + m + 1)
                    if e:
                        v.wait_ge(s["tanh"], 2 * (e - 1) + m + 1)
                        v.wait_ge(s["glu"], 2 * (e - 1) + m + 1)
                    nc.vector.tensor_scalar(gate[:, m, :], ps[:, 2 + m, :], b_up[:, e, m:m + 1], LIMIT, ALU.add,
                                            ALU.min).then_inc(s["gate_b"], 1)
                for m in range(2):
                    v.wait_ge(s["gu"], 4 * e + 2 + m + 1)
                    if e:
                        v.wait_ge(s["act"], 2 * (e - 1) + m + 1)
                    nc.vector.tensor_scalar(up[:, m, :], ps[:, 4 + m, :], b_up[:, e, 2 + m:3 + m], -LIMIT, ALU.add,
                                            ALU.max).then_inc(s["up_b"], 1)
                    v.wait_ge(s["up_b"], 2 * e + m + 1)
                    nc.vector.tensor_scalar(up[:, m, :], up[:, m, :], LIMIT, 1.0, ALU.min,
                                            ALU.add).then_inc(s["up_c"], 1)
                for m in range(2):
                    v.wait_ge(s["tanh"], 2 * e + m + 1)
                    if e:
                        v.wait_ge(s["a_lo"], e)
                    nc.vector.scalar_tensor_tensor(out=glu[:, m, :], in0=th[:, m, :], scalar=1.0, in1=gate[:, m, :],
                                                   op0=ALU.add, op1=ALU.mult).then_inc(s["glu"], 1)
                    v.wait_ge(s["glu"], 2 * e + m + 1)
                    v.wait_ge(s["up_c"], 2 * e + m + 1)
                    nc.vector.scalar_tensor_tensor(out=glu[:, m, :], in0=glu[:, m, :], scalar=0.5, in1=up[:, m, :],
                                                   op0=ALU.mult, op1=ALU.mult).then_inc(s["act"], 1)
                if e == 0:
                    v.wait_ge(s["bias"], 1)
                    nc.vector.tensor_tensor(acc[:].rearrange("p a b -> p (a b)"), acc[:].rearrange("p a b -> p (a b)"),
                                            ps[:, 0:2, :].rearrange("p a b -> p (a b)"), ALU.add).then_inc(s["bias_added"], 1)
                    v.wait_ge(s["bias_added"], 1)
                    v.wait_ge(s["wc"], 1)
                if e >= 2:
                    combine(e - 2)
            combine(E_N - 2)
            combine(E_N - 1)

        @block.tensor
        def _(pe):
            def product(out, lh, ll, rh, rl):
                terms = [t for k in range(DC) for t in ((lh(k), rh(k)), (lh(k), rl(k)), (ll(k), rh(k)))]
                for i, (a, b) in enumerate(terms):
                    last = nc.tensor.matmul(out, a, b, start=(i == 0), stop=(i == len(terms) - 1))
                return last

            pe.wait_ge(s["normed"], 1)
            for q in range(MQ):
                for c in range(DC):
                    last = nc.tensor.transpose(ps[:, c, q * P:(q + 1) * P], xn[:, q, c * P:(c + 1) * P], ident[:])
            last.then_inc(s["xT"], 1)
            pe.wait_ge(s["wc"], 1)
            for q in range(MQ):
                last = nc.tensor.transpose(ps[0:E_N, 6, q * P:(q + 1) * P], wc[:, q, :], ident[:])
            last.then_inc(s["wcT"], 1)
            pe.wait_ge(s["x_lo"], 1)

            def gate_up(e):
                pe.wait_ge(s["w_lo"], e + 1)
                for m in range(4):
                    if e:
                        pe.wait_ge(s["gate_b"] if m < 2 else s["up_b"], 2 * (e - 1) + m % 2 + 1)
                    product(ps[:, 2 + m, :], lambda k: w_h[:, e % SLOTS, k * 2 * D + m * P:k * 2 * D + (m + 1) * P],
                            lambda k: w_l[:, e % SLOTS, k * 2 * D + m * P:k * 2 * D + (m + 1) * P],
                            lambda k: x_h[:, k, :], lambda k: x_l[:, k, :]).then_inc(s["gu"], 1)

            def down(e):
                pe.wait_ge(s["a_lo"], e + 1)
                for q in range(MQ):
                    if e == 0:
                        pe.wait_ge(s["bias_added"], 1)
                    else:
                        pe.wait_ge(s["acc"], MQ * (e - 1) + q + 1)
                    product(ps[:, (6, 7, 0, 1)[q], 0:D], lambda k: a_h[:, e % 2, k, q * P:(q + 1) * P],
                            lambda k: a_l[:, e % 2, k, q * P:(q + 1) * P],
                            lambda k: w_h[:, e % SLOTS, 4 * D + k * D:4 * D + (k + 1) * D],
                            lambda k: w_l[:, e % SLOTS, 4 * D + k * D:4 * D + (k + 1) * D]).then_inc(s["down"], 1)

            for e in range(E_N):
                gate_up(e)
                if e == 0:
                    pe.wait_ge(s["wcT_copy"], 1)
                    for q in range(MQ):
                        last = nc.tensor.matmul(ps[:, q // 2, (q % 2) * D:(q % 2 + 1) * D], wcT[:, q, :], b_dn[:], start=True,
                                                stop=True)
                    last.then_inc(s["bias"], 1)
                if e >= 2:
                    down(e - 2)
            down(E_N - 2)
            down(E_N - 1)


def program(nc, io):
    with ExitStack() as ctx:
        consts, W = Names(), Names()

        def sb(name, shape, dt=F32):
            return ctx.enter_context(nc.sbuf_tensor(name, shape, dt))

        consts.ident, consts.ones, consts.halves = sb("ident", [P, P]), sb("ones", [P, P]), sb("halves", [P, P])
        consts.halfpow = sb("half_powers", [P, 2, 4])
        W.in_h, W.in_l = sb("Win_hi", [P, DC, 2 * DI], F32R), sb("Win_lo", [P, DC, 2 * DI], F32R)
        W.l_h, W.l_l = sb("Wl_hi", [P, IC, DI], F32R), sb("Wl_lo", [P, IC, DI], F32R)
        W.v_h, W.v_l = sb("Wv_hi", [P, IC, DI], F32R), sb("Wv_lo", [P, IC, DI], F32R)
        W.out_h, W.out_l = sb("Wout_hi", [P, IC, D], F32R), sb("Wout_lo", [P, IC, D], F32R)
        zeroed = ctx.enter_context(nc.semaphore("ident_zeroed"))
        made = ctx.enter_context(nc.semaphore("consts_made"))
        with nc.Block() as block:
            @block.gpsimd
            def _(pool):
                nc.gpsimd.memset(consts.ident[:], 0.0).then_inc(zeroed, 1)
                nc.gpsimd.memset(consts.ones[:], 1.0)
                nc.gpsimd.memset(consts.halves[:], 0.5)
                nc.gpsimd.memset(consts.halfpow[:, 0, :], 0.5)
                nc.gpsimd.memset(consts.halfpow[:, 1, :], -0.5)
                pool.wait_ge(zeroed, 1)
                nc.gpsimd.affine_select(out=consts.ident[:], in_=consts.ident[:], compare_op=ALU.not_equal, fill=1.0,
                                        base=0, pattern=[[-1, P]], channel_multiplier=1).then_inc(made, 1)
                pool.wait_ge(made, 1)
        part_a(nc, W, io, consts)
        part_b(nc, W, io, consts)
        part_c(nc, io, consts)


def kernel(x, x_txt, L0_tok_W, L0_tok_b, L0_txt_weight, L0_attn_wq, L0_attn_wk, L0_attn_wv, L0_ffn_w_up,
           L0_ffn_w_down, L1_attn_omega, L1_attn_Win, L1_attn_Wl, L1_attn_bl, L1_attn_Wv, L1_attn_bv, L1_attn_Wout,
           L1_ffn_router_indices, L1_ffn_routing_weights, L1_ffn_gate_up_proj, L1_ffn_gate_up_proj_bias,
           L1_ffn_down_proj, L1_ffn_down_proj_bias):
    import numpy as np
    import concourse.bacc as bacc
    from concourse.bass_utils import run_bass_kernel_spmd as run

    def rows(a):
        a = np.asarray(a)
        c = a.shape[0] // P
        return a.reshape(c, P, -1).transpose(1, 0, 2).reshape(P, -1)

    x = np.asarray(x)
    pat = x.reshape(G, 2, 3, 8, 16, 8, 16).transpose(0, 2, 4, 6, 1, 3, 5).reshape(G, KPC, P, P).transpose(0, 2, 1, 3)
    vectors = np.stack([np.asarray(a).reshape(IC, P).T for a in (L1_attn_omega, L1_attn_bl, L1_attn_bv)], axis=1)
    gu = np.asarray(L1_ffn_gate_up_proj)
    gu = np.concatenate([gu[..., 0::2], gu[..., 1::2]], axis=-1)
    gub = np.asarray(L1_ffn_gate_up_proj_bias)
    gub = np.concatenate([gub[..., 0::2], gub[..., 1::2]], axis=-1)
    dn = np.asarray(L1_ffn_down_proj)
    experts = np.concatenate([np.stack([rows(gu[e]) for e in range(E_N)]),
                              np.stack([rows(dn[e]) for e in range(E_N)])], axis=-1)
    arrays = {
        "patches": pat, "ids": np.asarray(x_txt).reshape(G, 2, P).transpose(0, 2, 1),
        "tokW": rows(L0_tok_W), "tokb": np.broadcast_to(np.asarray(L0_tok_b), (P, D)), "table": L0_txt_weight,
        "wq": rows(L0_attn_wq), "wk": rows(L0_attn_wk), "wvT": rows(np.asarray(L0_attn_wv).T),
        "upT": rows(np.asarray(L0_ffn_w_up).T), "downT": rows(np.asarray(L0_ffn_w_down).T),
        "vectors": vectors, "WinT": rows(np.asarray(L1_attn_Win).T), "WlT": rows(np.asarray(L1_attn_Wl).T),
        "WvT": rows(np.asarray(L1_attn_Wv).T), "WoutT": rows(np.asarray(L1_attn_Wout).T),
        "picked": np.asarray(L1_ffn_router_indices).reshape(MT // P, P, 2).transpose(1, 0, 2),
        "routing": np.asarray(L1_ffn_routing_weights).reshape(MT // P, P, E_N).transpose(1, 0, 2),
        "up_bias": gub.reshape(E_N, 4, P).transpose(2, 0, 1), "down_bias": L1_ffn_down_proj_bias,
        "experts": experts,
    }
    nc = bacc.Bacc("TRN2", target_bir_lowering=False, num_devices=1)
    io, ins = {}, {}
    for name, a in arrays.items():
        a = np.ascontiguousarray(np.asarray(a))
        ins[f"in_{name}"] = a
        io[name] = nc.dram_tensor(f"in_{name}", a.shape, mybir.dt.from_np(a.dtype), kind="ExternalInput").ap()
    io["wq"] = io["wq"].rearrange("p (k n) -> p k n", k=DC)
    io["wk"] = io["wk"].rearrange("p (k n) -> p k n", k=DC)
    io["h2"] = nc.dram_tensor("layer0_out", (NB, T, D), F32, kind="Internal").ap()
    io["out"] = nc.dram_tensor("out_dram", (NB, T, D), F32, kind="ExternalOutput").ap()
    program(nc, io)
    r = run(nc, [ins], core_ids=[0])
    return r.results[0]["out_dram"]
```
